# Optimizing a Trainium2 kernel written in Bass

```python
import numpy as np
import jax
import jax.numpy as jnp

def _softmax(x, axis=-1):
    return jax.nn.softmax(x, axis=axis)

def _gelu(x):
    return jax.nn.gelu(x, approximate=True)

def _silu(x):
    return jax.nn.silu(x)

def _sigmoid(x):
    return jax.nn.sigmoid(x)

def _layernorm(x, axis=-1, eps=1e-05):
    m = jnp.mean(x, axis=axis, keepdims=True)
    v = jnp.var(x, axis=axis, keepdims=True)
    return (x - m) / jnp.sqrt(v + eps)

def _scatter_add(tgt, idx, src, axis=0):
    return tgt.at[idx].add(src)

def _segment_sum(src, seg, n):
    return jax.ops.segment_sum(src, seg, n)
kernel_name = 'mk_recurrent_d1_jaxref_r8_78c6a6'

def setup_inputs(seed: int=0):
    np.random.seed(seed)
    _w = jnp.asarray

    def _L0_attn_setup():
        import jax, jax.numpy as jnp
        import numpy as np
        B, S, D, H, DH = (4, 256, 128, 16, 64)
        SCALE = 1.0 / DH ** 0.5
        LN_EPS = 1e-05

        def _layer_norm(x, gamma, beta):
            mu = jnp.mean(x, axis=-1, keepdims=True)
            var = jnp.mean(jnp.square(x - mu), axis=-1, keepdims=True)
            return gamma * (x - mu) * jax.lax.rsqrt(var + LN_EPS) + beta
        key = jax.random.key(seed)
        ks = jax.random.split(key, 5)
        h = jax.random.normal(ks[0], (B, S, D), dtype=jnp.float32)
        Wq = SCALE * jax.random.normal(ks[1], (D, H * DH), dtype=jnp.float32)
        Wk = SCALE * jax.random.normal(ks[2], (D, H * DH), dtype=jnp.float32)
        Wv = SCALE * jax.random.normal(ks[3], (D, H * DH), dtype=jnp.float32)
        Wo = SCALE * jax.random.normal(ks[4], (H * DH, D), dtype=jnp.float32)
        gamma = jnp.ones((D,), dtype=jnp.float32)
        beta = jnp.zeros((D,), dtype=jnp.float32)
        return {'h': h, 'Wq': Wq, 'Wk': Wk, 'Wv': Wv, 'Wo': Wo, 'gamma': gamma, 'beta': beta}
    _L0_attn_in = _L0_attn_setup()

    def _L0_ffn_setup():
        import jax, jax.numpy as jnp
        import numpy as np
        H = 128
        I = 352
        E = 8
        TOP_K = 2

        def _moe(hidden_states, router_w, gate_w, up_w, down_w):
            B, S, Hd = hidden_states.shape
            x = hidden_states.reshape(-1, Hd)
            logits = x @ router_w.T
            probs = jax.nn.softmax(logits.astype(jnp.float32), axis=-1)
            top_w, top_idx = jax.lax.top_k(probs, TOP_K)
            top_w = top_w.astype(x.dtype)
            onehot = jax.nn.one_hot(top_idx, E, dtype=x.dtype)
            w_te = jnp.einsum('tk,tke->te', top_w, onehot)
            g = jnp.einsum('th,eih->tei', x, gate_w)
            u = jnp.einsum('th,eih->tei', x, up_w)
            h = jax.nn.silu(g) * u
            y = jnp.einsum('tei,ehi,te->th', h, down_w, w_te)
            return y.reshape(B, S, Hd)
        key = jax.random.key(seed)
        ks = jax.random.split(key, 5)
        s = 0.02
        return {'hidden_states': jax.random.normal(ks[0], (2, 128, H), dtype=jnp.float32), 'router_w': jax.random.normal(ks[1], (E, H), dtype=jnp.float32) * s, 'gate_w': jax.random.normal(ks[2], (E, I, H), dtype=jnp.float32) * s, 'up_w': jax.random.normal(ks[3], (E, I, H), dtype=jnp.float32) * s, 'down_w': jax.random.normal(ks[4], (E, H, I), dtype=jnp.float32) * s}
    _L0_ffn_in = _L0_ffn_setup()
    _d = {'L0_attn_h': _L0_attn_in['h'], 'L0_attn_Wq': _L0_attn_in['Wq'], 'L0_attn_Wk': _L0_attn_in['Wk'], 'L0_attn_Wv': _L0_attn_in['Wv'], 'L0_attn_Wo': _L0_attn_in['Wo'], 'L0_attn_gamma': _L0_attn_in['gamma'], 'L0_attn_beta': _L0_attn_in['beta'], 'L0_ffn_router_w': _L0_ffn_in['router_w'], 'L0_ffn_gate_w': _L0_ffn_in['gate_w'], 'L0_ffn_up_w': _L0_ffn_in['up_w'], 'L0_ffn_down_w': _L0_ffn_in['down_w']}
    _x0 = _d['L0_attn_h']
    _d['L0_attn_h'] = jax.random.normal(jax.random.fold_in(jax.random.key(seed), 1), (4, 512, 128), dtype=_x0.dtype)
    del _x0
    return _d

def reference(L0_attn_h, L0_attn_Wq, L0_attn_Wk, L0_attn_Wv, L0_attn_Wo, L0_attn_gamma, L0_attn_beta, L0_ffn_router_w, L0_ffn_gate_w, L0_ffn_up_w, L0_ffn_down_w):

    def _L0_attn_ref(h, Wq, Wk, Wv, Wo, gamma, beta):
        import jax, jax.numpy as jnp
        import numpy as np
        B, S, D, H, DH = (4, 256, 128, 16, 64)
        SCALE = 1.0 / DH ** 0.5
        LN_EPS = 1e-05

        def _layer_norm(x, gamma, beta):
            mu = jnp.mean(x, axis=-1, keepdims=True)
            var = jnp.mean(jnp.square(x - mu), axis=-1, keepdims=True)
            return gamma * (x - mu) * jax.lax.rsqrt(var + LN_EPS) + beta
        b, s, d = h.shape
        q = (h @ Wq).reshape(b, s, H, DH)
        k = (h @ Wk).reshape(b, s, H, DH)
        v = (h @ Wv).reshape(b, s, H, DH)
        scores = jnp.einsum('bind,bjnd->bijn', q, k) * SCALE
        probs = jax.nn.softmax(scores, axis=2)
        attn_vec = jnp.einsum('bijn,bjnd->bind', probs, v).reshape(b, s, H * DH)
        attn_out = attn_vec @ Wo
        return _layer_norm(h + attn_out, gamma, beta)

    def _L0_ffn_ref(hidden_states, router_w, gate_w, up_w, down_w):
        import jax, jax.numpy as jnp
        import numpy as np
        H = 128
        I = 352
        E = 8
        TOP_K = 2

        def _moe(hidden_states, router_w, gate_w, up_w, down_w):
            B, S, Hd = hidden_states.shape
            x = hidden_states.reshape(-1, Hd)
            logits = x @ router_w.T
            probs = jax.nn.softmax(logits.astype(jnp.float32), axis=-1)
            top_w, top_idx = jax.lax.top_k(probs, TOP_K)
            top_w = top_w.astype(x.dtype)
            onehot = jax.nn.one_hot(top_idx, E, dtype=x.dtype)
            w_te = jnp.einsum('tk,tke->te', top_w, onehot)
            g = jnp.einsum('th,eih->tei', x, gate_w)
            u = jnp.einsum('th,eih->tei', x, up_w)
            h = jax.nn.silu(g) * u
            y = jnp.einsum('tei,ehi,te->th', h, down_w, w_te)
            return y.reshape(B, S, Hd)
        return _moe(hidden_states, router_w, gate_w, up_w, down_w)
    x = L0_attn_h
    xn = _layernorm(x, axis=-1)
    s = _L0_attn_ref(xn, L0_attn_Wq, L0_attn_Wk, L0_attn_Wv, L0_attn_Wo, L0_attn_gamma, L0_attn_beta)
    g = _silu(_L0_ffn_ref(xn, L0_ffn_router_w, L0_ffn_gate_w, L0_ffn_up_w, L0_ffn_down_w))
    x = x + s * g
    return x

_drawn_inputs = setup_inputs


def setup_inputs(seed=0):
    import zlib

    import numpy as np

    out = dict(_drawn_inputs(seed))
    spreads = {'L0_attn_gamma': (1.0, 0.6), 'L0_attn_beta': (0.0, 0.8)}
    factors = {'L0_attn_Wq': 8.0,
     'L0_attn_Wk': 8.0,
     'L0_attn_Wv': 8.0,
     'L0_attn_Wo': 8.0,
     'L0_ffn_router_w': 8.0,
     'L0_ffn_gate_w': 8.0,
     'L0_ffn_up_w': 8.0,
     'L0_ffn_down_w': 8.0}
    for name, (base, spread) in spreads.items():
        noise = np.random.default_rng([zlib.crc32(name.encode()), seed]).standard_normal(out[name].shape)
        drawn = base * np.exp(spread * noise) if base else spread * noise
        out[name] = jnp.asarray(drawn.astype(out[name].dtype))
    for name, factor in factors.items():
        out[name] = (out[name] * factor).astype(out[name].dtype)
    return out
```

```python
from contextlib import ExitStack

import concourse.bass as bass
from concourse import mybir

F32 = mybir.dt.float32
F32R = mybir.dt.float32r
ALU = mybir.AluOpType
ACT = mybir.ActivationFunctionType
AX_X = mybir.AxisListType.X

P = 128
D = 128
BATCH, SEQ = 4, 512
TOKENS = BATCH * SEQ
TILES = TOKENS // P
BT = SEQ // P
GROUPS = TILES // BT
HEADS, DH = 16, 64
PAIRS = HEADS // 2
UNITS = BATCH * PAIRS
SCALE = 1.0 / DH ** 0.5
LN_EPS = 1e-5
EXPERTS, INTER = 8, 352
CHUNKS = [128, 128, 96]
NC = len(CHUNKS)
A, B = 0, 1


def program(nc, x_in, wqkv_in, wo_in, gamma_in, beta_in, router_in, gate_up_in, down_in, out):
    ctx = ExitStack()
    with ctx:
        def sb(name, shape, dt=F32):
            return ctx.enter_context(nc.sbuf_tensor(name, shape, dt))

        def sem(name):
            return ctx.enter_context(nc.semaphore(name))

        x = sb("x", [P, TILES, D])
        xn = sb("xn", [P, TILES, D])
        scratch = sb("scratch", [P, TILES, D])
        ffn = sb("ffn", [P, TILES, D])
        xnT = sb("xnT", [D, TOKENS])
        xnT_hi = sb("xnT_hi", [D, TOKENS], F32R)
        xnT_lo = sb("xnT_lo", [D, TOKENS], F32R)
        ident = sb("ident", [P, P])
        gamma = sb("gamma", [P, D])
        beta = sb("beta", [P, D])
        row_sum = sb("row_sum", [P, TILES])
        mean = sb("mean", [P, TILES])
        sq_sum = sb("sq_sum", [P, TILES])
        var_eps = sb("var_eps", [P, TILES])
        rstd = sb("rstd", [P, TILES])
        minus_half = sb("minus_half", [P, TILES])
        router = sb("router", [D, EXPERTS])
        rank = sb("rank", [P, TILES, EXPERTS])
        prob = sb("prob", [P, TILES, EXPERTS])
        left = sb("left", [P, TILES, EXPERTS])
        eq = sb("eq", [P, TILES, EXPERTS])
        first = sb("first", [P, TILES, EXPERTS])
        second = sb("second", [P, TILES, EXPERTS])
        weight = sb("weight", [P, TILES * EXPERTS])
        best = sb("best", [P, TILES])
        gu_raw = sb("gu_raw", [D, 2, 2 * INTER])
        gu_hi = sb("gu_hi", [D, 2, 2 * INTER], F32R)
        gu_lo = sb("gu_lo", [D, 2, 2 * INTER], F32R)
        down = sb("down", [P, 2, NC, D])
        gate_act = sb("gate_act", [P, 2, SEQ])
        hidden = sb("hidden", [P, 2, NC, SEQ])
        wqkv = sb("wqkv", [D, PAIRS, 3, P])
        wqk_split = sb("wqk_split", [D, PAIRS, 2, 2, P], F32R)
        wo = sb("wo", [P, PAIRS, D])
        w_unit = sb("w_unit", [D, 2, 2, 2, P], F32R)
        x_unit = sb("x_unit", [D, 2, SEQ])
        q_hi = sb("q_hi", [P, SEQ], F32R)
        q_lo = sb("q_lo", [P, SEQ], F32R)
        k_hi = sb("k_hi", [P, SEQ], F32R)
        k_lo = sb("k_lo", [P, SEQ], F32R)
        q_stack = sb("q_stack", [P, 2, 2, SEQ], F32R)
        k_hi_stack = sb("k_hi_stack", [P, 2, 2, SEQ], F32R)
        k_lo_stack = sb("k_lo_stack", [P, 2, 2, SEQ], F32R)
        v_unit = sb("v_unit", [P, 2, BT, P])
        row_max = sb("row_max", [P, 2, BT])
        exp_bias = sb("exp_bias", [P, 2, BT])
        exp_sum = sb("exp_sum", [P, 2, BT])
        inv_sum = sb("inv_sum", [P, 2, BT])
        probs = sb("probs", [P, 2, BT, SEQ])
        probsT = sb("probsT", [P, 2, BT, SEQ])
        attnT = sb("attnT", [P, SEQ])

        bank = [ctx.enter_context(nc.psum_tensor(f"bank{i}", [P, SEQ], F32)) for i in range(3)]
        score = ctx.enter_context(nc.psum_tensor("score", [P, BT, SEQ], F32))
        extra = ctx.enter_context(nc.psum_tensor("extra", [P, SEQ], F32))
        misc = [bank[0], bank[1]]
        tr_bank = [bank[2], extra]
        gate_bank = [score[:, 0, :], score[:, 1, :]]
        up_bank = [score[:, 2, :], score[:, 3, :]]
        y_bank = [bank[0], bank[1]]

        x_loaded = [sem(f"x_loaded{g}") for g in range(GROUPS)]
        router_loaded, const_loaded, attn_w_loaded = sem("router_loaded"), sem("const_loaded"), sem("attn_w_loaded")
        gu_loaded = [sem("gu_loaded0"), sem("gu_loaded1")]
        down_loaded = [sem("down_loaded0"), sem("down_loaded1")]
        ident_zero, ident_ready, consts_ready = sem("ident_zero"), sem("ident_ready"), sem("consts_ready")
        stat_step, var_ready, rstd_ready, xn_ready = sem("stat_step"), sem("var_ready"), sem("rstd_ready"), sem("xn_ready")
        xnT_ready, xnT_hi_ready, xnT_f32_ready, xnT_lo_ready = sem("xnT_ready"), sem("xnT_hi_ready"), sem("xnT_f32_ready"), sem("xnT_lo_ready")
        logits_ready, shifted_ready, router_exp_ready, route_step = sem("logits_ready"), sem("shifted_ready"), sem("router_exp_ready"), sem("route_step")
        wqk_hi_ready, wqk_lo_ready = sem("wqk_hi_ready"), sem("wqk_lo_ready")
        gu_hi_ready, gu_lo_ready = sem("gu_hi_ready"), sem("gu_lo_ready")
        gate_ready, up_ready, silu_ready, hidden_ready = sem("gate_ready"), sem("up_ready"), sem("silu_ready"), sem("hidden_ready")
        y_ready, ffn_zero, ffn_added, ffn_ready = sem("y_ready"), sem("ffn_zero"), sem("ffn_added"), sem("ffn_ready")
        unit_loaded = [sem("unit_loaded0"), sem("unit_loaded1")]
        stack_loaded = [sem("stack_loaded0"), sem("stack_loaded1")]
        q_ready, k_ready, v_ready = sem("q_ready"), sem("k_ready"), sem("v_ready")
        q_hi_ready, q_lo_ready, k_hi_ready, k_lo_ready, v_copied = (
            sem("q_hi_ready"), sem("q_lo_ready"), sem("k_hi_ready"), sem("k_lo_ready"), sem("v_copied"))
        scores_ready, max_ready, bias_ready, exp_ready = sem("scores_ready"), sem("max_ready"), sem("bias_ready"), sem("exp_ready")
        inv_ready, probs_ready = sem("inv_ready"), sem("probs_ready")
        probsT_ready, copied_by_act, copied_by_dve = sem("probsT_ready"), sem("copied_by_act"), sem("copied_by_dve")
        attn_ready, attn_copied, proj_ready, proj_added = sem("attn_ready"), sem("attn_copied"), sem("proj_ready"), sem("proj_added")
        fin_step, fin_var_ready, fin_rstd_ready, fin_ready = sem("fin_step"), sem("fin_var_ready"), sem("fin_rstd_ready"), sem("fin_ready")
        pool_turn = sem("pool_turn")
        stored = sem("stored")

        def group(t, g):
            return t[:, bass.ds(g * BT, BT), :] if not isinstance(g, int) else t[:, g * BT:(g + 1) * BT, :]

        def cols(t, g, n):
            return t[:, bass.ds(g * n, n)] if not isinstance(g, int) else t[:, g * n:(g + 1) * n]

        def spread(t, n):
            return t.unsqueeze(2).to_broadcast([t.shape[0], t.shape[1], n])

        block = ctx.enter_context(nc.Block())

        def over_units(eng, body):
            body(0, 0, 0)
            with eng.Fori(0, UNITS // 2 - 1) as i:
                body(2 * i + 1, 1, i)
                body(2 * i + 2, 0, i + 1)
            body(UNITS - 1, 1, UNITS // 2 - 1)

        def over_experts(eng, body):
            body(0, 0, 0)
            with eng.Fori(0, EXPERTS // 2 - 1) as i:
                body(2 * i + 1, 1, i)
                body(2 * i + 2, 0, i + 1)
            body(EXPERTS - 1, 1, EXPERTS // 2 - 1)

        def is_first(u):
            return isinstance(u, int) and u == 0

        def is_last(u, n):
            return isinstance(u, int) and u == n - 1

        @block.sync
        def _(sp):
            for g in range(GROUPS):
                sp.dma_start(group(x, g), group(x_in, g)).then_inc(x_loaded[g], 16)
            sp.dma_start(router[:], router_in).then_inc(router_loaded, 16)

            def load_expert(e, slot):
                sp.dma_start(gu_raw[:, slot, :], gu_dram(e)).then_inc(gu_loaded[slot], 16)
                for c in range(NC):
                    sp.dma_start(down[0:CHUNKS[c], slot, c, :], down_dram(e, c)).then_inc(down_loaded[slot], 16)

            def gu_dram(e):
                return gate_up_in[bass.ds(e, 1), :, :].rearrange("e p n -> (e p) n") if not isinstance(e, int) else gate_up_in[e, :, :]

            def down_dram(e, c):
                return down_in[bass.ds(e * INTER + c * P, CHUNKS[c]), :] if not isinstance(e, int) else \
                    down_in[e * INTER + c * P:e * INTER + c * P + CHUNKS[c], :]

            load_expert(0, 0)
            load_expert(1, 1)
            sp.dma_start(wqkv[:], wqkv_in).then_inc(attn_w_loaded, 16)
            sp.dma_start(wo[:], wo_in).then_inc(attn_w_loaded, 16)
            sp.dma_start(gamma[:], gamma_in.partition_broadcast(P)).then_inc(const_loaded, 16)
            sp.dma_start(beta[:], beta_in.partition_broadcast(P)).then_inc(const_loaded, 16)
            with sp.Fori(0, EXPERTS // 2 - 1) as i:
                for slot in range(2):
                    e = 2 * i + 2 + slot
                    sp.wait_ge(y_ready, BATCH * (e - 1))
                    load_expert(e, slot)

            def load_unit(u, slot):
                b, pair = u // PAIRS, u % PAIRS
                if isinstance(u, int):
                    w_src, x_src = wqk_split[:, pair], xnT[:, b * SEQ:(b + 1) * SEQ]
                else:
                    w_src = wqk_split[:, bass.ds(pair, 1)].rearrange("p o a s c -> p (o a) s c")
                    x_src = xnT[:, bass.ds(b * SEQ, SEQ)]
                if not isinstance(u, int) or u >= 2:
                    sp.wait_ge(v_ready, u - 1)
                sp.dma_start(w_unit[:, slot].bitcast(F32), w_src.bitcast(F32)).then_inc(unit_loaded[slot], 16)
                sp.dma_start(x_unit[:, slot, :], x_src).then_inc(unit_loaded[slot], 16)

            def stack_unit(u, slot):
                if not isinstance(u, int) or u >= 2:
                    sp.wait_ge(scores_ready, 2 * BT * (u - 1))
                for ready, src, stacks in ((q_hi_ready, q_hi, [q_stack[0:DH, slot]]),
                                           (q_lo_ready, q_lo, [q_stack[DH:P, slot]]),
                                           (k_hi_ready, k_hi, [k_hi_stack[0:DH, slot], k_hi_stack[DH:P, slot]]),
                                           (k_lo_ready, k_lo, [k_lo_stack[0:DH, slot], k_lo_stack[DH:P, slot]])):
                    sp.wait_ge(ready, u + 1)
                    for dst in stacks:
                        for h in (A, B):
                            sp.dma_start(dst[:, h, :].bitcast(F32), src[h * DH:(h + 1) * DH, :].bitcast(F32)).then_inc(stack_loaded[slot], 16)

            sp.wait_ge(wqk_lo_ready, 1)
            sp.wait_ge(xnT_f32_ready, GROUPS)
            load_unit(0, 0)
            load_unit(1, 1)
            stack_unit(0, 0)

            load_unit(2, 0)
            stack_unit(1, 1)
            with sp.Fori(0, UNITS // 2 - 2) as i:
                load_unit(2 * i + 3, 1)
                stack_unit(2 * i + 2, 0)
                load_unit(2 * i + 4, 0)
                stack_unit(2 * i + 3, 1)
            load_unit(UNITS - 1, 1)
            stack_unit(UNITS - 2, 0)
            stack_unit(UNITS - 1, 1)

            with sp.Fori(0, GROUPS) as g:
                sp.wait_ge(fin_ready, g + 1)
                sp.dma_start(group(out, g), group(scratch, g)).then_inc(stored, 16)
            sp.wait_ge(stored, 16 * GROUPS)

        @block.gpsimd
        def _(pool):
            nc.gpsimd.memset(ident[:], 0.0).then_inc(ident_zero, 1)
            nc.gpsimd.memset(minus_half[:], -0.5).then_inc(consts_ready, 1)
            pool.wait_ge(ident_zero, 1)
            nc.gpsimd.affine_select(out=ident[:], in_=ident[:], compare_op=ALU.not_equal, fill=1.0,
                                    base=0, pattern=[[-1, P]], channel_multiplier=1).then_inc(ident_ready, 1)
            pool.wait_ge(consts_ready, 1)
            with pool.Fori(0, GROUPS) as g:
                pool.wait_ge(var_ready, g + 1)
                nc.gpsimd.tensor_tensor(cols(rstd, g, BT), cols(var_eps, g, BT), cols(minus_half, g, BT),
                                        ALU.pow).then_inc(rstd_ready, 1)
            for e in range(EXPERTS):
                nc.gpsimd.memset(rank[:, :, e], float(EXPERTS - e)).then_inc(consts_ready, 1)
            nc.gpsimd.memset(ffn[:], 0.0).then_inc(ffn_zero, 1)

            def normalise(h, kind):
                for it in range(BT):
                    if it % 2 == 0:
                        pool.wait_ge(inv_ready, 2 * h + it // 2 + 1)
                        pool.sem_inc(pool_turn, 1)
                    nc.gpsimd.tensor_scalar(probs[:, kind, it, :], probs[:, kind, it, :],
                                            inv_sum[:, kind, it:it + 1], 1.0, ALU.mult, ALU.mult)\
                        .then_inc(probs_ready, 1)

            with pool.Fori(0, UNITS) as u:
                normalise(2 * u, A)
                normalise(2 * u + 1, B)

            with pool.Fori(0, GROUPS) as g:
                pool.wait_ge(fin_var_ready, g + 1)
                nc.gpsimd.tensor_tensor(cols(rstd, g, BT), cols(var_eps, g, BT), cols(minus_half, g, BT),
                                        ALU.pow).then_inc(fin_rstd_ready, 1)

        @block.scalar
        def _(act):
            for g in range(GROUPS):
                act.wait_ge(xnT_ready, g + 1)
                nc.scalar.activation(cols(xnT_hi, g, SEQ), score[:, g, :], ACT.Copy).then_inc(xnT_hi_ready, 1)
                nc.scalar.activation(cols(xnT, g, SEQ), score[:, g, :], ACT.Copy).then_inc(xnT_f32_ready, 1)
            act.wait_ge(shifted_ready, 1)
            nc.scalar.activation(prob[:], left[:], ACT.Exp).then_inc(router_exp_ready, 1)

            def split_hi(e, slot):
                act.wait_ge(gu_loaded[slot], 16 * ((e // 2) + 1))
                if not isinstance(e, int) or e >= 2:
                    act.wait_ge(y_ready, BATCH * (e - 1))
                nc.scalar.activation(gu_hi[:, slot, :], gu_raw[:, slot, :], ACT.Copy).then_inc(gu_hi_ready, 1)

            split_hi(0, 0)
            act.wait_ge(attn_w_loaded, 32)
            nc.scalar.activation(wqk_split[:, :, :, 0, :], wqkv[:, :, 0:2, :], ACT.Copy).then_inc(wqk_hi_ready, 1)

            def expert(e, slot, half):
                for tb in range(BATCH):
                    for c in range(NC):
                        n = e * (BATCH * NC) + tb * NC + c
                        ln = n if isinstance(n, int) else None
                        act.wait_ge(gate_ready, n + 1)
                        if ln is None or ln >= 2:
                            act.wait_ge(hidden_ready, n - 1)
                        m = CHUNKS[c]
                        k = (tb * NC + c) % 2
                        nc.scalar.activation(gate_act[0:m, k, :], gate_bank[k][0:m, :], ACT.Silu)\
                            .then_inc(silu_ready, 1)
                    if tb == 1 and not is_last(e, EXPERTS):
                        split_hi(e + 1, 1 - slot)

            over_experts(act, expert)

            with act.Fori(0, GROUPS) as g:
                act.wait_ge(ffn_added, TILES * (EXPERTS - 1) + BT * (g + 1))
                nc.scalar.activation(group(ffn, g), group(ffn, g), ACT.Silu).then_inc(ffn_ready, 1)

            def copy_hi(u, ready, b, hi, hi_ready):
                act.wait_ge(ready, u + 1)
                nc.scalar.activation(hi[:], misc[b][:], ACT.Copy).then_inc(hi_ready, 1)

            def exps(u, kind, its):
                h = 2 * u + kind
                act.wait_ge(bias_ready, 2 * h + its[0] // 2 + 1)
                if its[0] == 0 and (not isinstance(h, int) or h >= 2):
                    act.wait_ge(probsT_ready, BT * (h - 1))
                for it in its:
                    nc.scalar.activation(probs[:, kind, it, :], score[:, it, :], ACT.Exp,
                                         bias=exp_bias[:, kind, it:it + 1], scale=SCALE,
                                         accum_out=exp_sum[:, kind, it:it + 1]).then_inc(exp_ready, 1)

            def copy_probsT(u, kind):
                h = 2 * u + kind
                if not is_first(u):
                    act.wait_ge(attn_ready, u)
                for jt in (0, 2):
                    act.wait_ge(probsT_ready, BT * h + jt + 1)
                    nc.scalar.activation(probsT[:, kind, jt, :], tr_bank[0][:], ACT.Copy).then_inc(copied_by_act, 1)

            copy_hi(0, q_ready, Q_BANK[0], q_hi, q_hi_ready)
            copy_hi(0, k_ready, K_BANK[0], k_hi, k_hi_ready)
            exps(0, A, (0, 1))
            exps(0, A, (2, 3))

            def unit(u, slot, half):
                nxt = 1 - slot
                if not is_last(u, UNITS):
                    act.wait_ge(stack_loaded[slot], 16 * STACK_DMAS * (half + 1))
                    copy_hi(u + 1, q_ready, Q_BANK[nxt], q_hi, q_hi_ready)
                exps(u, B, (0, 1))
                if not is_last(u, UNITS):
                    copy_hi(u + 1, k_ready, K_BANK[nxt], k_hi, k_hi_ready)
                exps(u, B, (2, 3))
                copy_probsT(u, A)
                if not is_last(u, UNITS):
                    exps(u + 1, A, (0, 1))
                    exps(u + 1, A, (2, 3))
                copy_probsT(u, B)
                act.wait_ge(attn_ready, u + 1)
                if not is_first(u):
                    act.wait_ge(proj_ready, u)
                nc.scalar.activation(attnT[:], misc[PV_BANK[slot]][:], ACT.Copy).then_inc(attn_copied, 1)

            over_units(act, unit)

        @block.vector
        def _(dve):
            def layer_norm(g, src, dst, var_sem, rstd_sem, step_sem, base):
                nc.vector.reduce_sum(cols(row_sum, g, BT), group(src, g), AX_X).then_inc(step_sem, 1)
                dve.wait_ge(step_sem, base + 1)
                nc.vector.tensor_scalar(cols(mean, g, BT), cols(row_sum, g, BT), 1.0 / D, None, ALU.mult)\
                    .then_inc(step_sem, 1)
                dve.wait_ge(step_sem, base + 2)
                nc.vector.tensor_tensor(group(dst, g), group(src, g), spread(cols(mean, g, BT), D),
                                        ALU.subtract).then_inc(step_sem, 1)
                dve.wait_ge(step_sem, base + 3)
                nc.vector.tensor_tensor(group(scratch, g), group(dst, g), group(dst, g), ALU.mult)\
                    .then_inc(step_sem, 1)
                dve.wait_ge(step_sem, base + 4)
                nc.vector.reduce_sum(cols(sq_sum, g, BT), group(scratch, g), AX_X).then_inc(step_sem, 1)
                dve.wait_ge(step_sem, base + 5)
                nc.vector.tensor_scalar(cols(var_eps, g, BT), cols(sq_sum, g, BT), 1.0 / D, LN_EPS,
                                        ALU.mult, ALU.add).then_inc(var_sem, 1)
                dve.wait_ge(rstd_sem, g + 1)

            for g in range(GROUPS):
                dve.wait_ge(x_loaded[g], 16)
                layer_norm(g, x, xn, var_ready, rstd_ready, stat_step, 5 * g)
                nc.vector.tensor_tensor(group(xn, g), group(xn, g), spread(cols(rstd, g, BT), D), ALU.mult)\
                    .then_inc(xn_ready, 1)
            for g in range(GROUPS):
                dve.wait_ge(xnT_f32_ready, g + 1)
                nc.vector.tensor_tensor(cols(xnT_lo, g, SEQ), score[:, g, :], cols(xnT_hi, g, SEQ).bitcast(F32),
                                        ALU.subtract).then_inc(xnT_lo_ready, 1)

            def split_lo(e, slot):
                dve.wait_ge(gu_hi_ready, e + 1)
                nc.vector.tensor_tensor(gu_lo[:, slot, :], gu_raw[:, slot, :], gu_hi[:, slot, :].bitcast(F32),
                                        ALU.subtract).then_inc(gu_lo_ready, 1)

            step = [0]

            def link(instruction):
                step[0] += 1
                instruction.then_inc(route_step, 1)
                dve.wait_ge(route_step, step[0])

            lg = bank[0][:, 0:TILES * EXPERTS].rearrange("p (t e) -> p t e", e=EXPERTS)
            dve.wait_ge(logits_ready, 1)
            link(nc.vector.reduce_max(best[:], lg, AX_X))
            nc.vector.tensor_tensor(left[:], lg, spread(best[:], EXPERTS), ALU.subtract).then_inc(shifted_ready, 1)
            dve.wait_ge(router_exp_ready, 1)
            split_lo(0, 0)
            link(nc.vector.reduce_sum(best[:], prob[:], AX_X))
            link(nc.vector.reciprocal(best[:], best[:]))
            link(nc.vector.tensor_tensor(prob[:], prob[:], spread(best[:], EXPERTS), ALU.mult))
            dve.wait_ge(consts_ready, 1 + EXPERTS)

            def pick(values, chosen):
                link(nc.vector.reduce_max(best[:], values, AX_X))
                link(nc.vector.tensor_tensor(eq[:], values, spread(best[:], EXPERTS), ALU.is_equal))
                link(nc.vector.tensor_tensor(eq[:], eq[:], rank[:], ALU.mult))
                link(nc.vector.reduce_max(best[:], eq[:], AX_X))
                link(nc.vector.tensor_tensor(chosen, eq[:], spread(best[:], EXPERTS), ALU.is_equal))

            pick(prob[:], first[:])
            link(nc.vector.scalar_tensor_tensor(out=left[:], in0=first[:], scalar=-2.0, in1=prob[:],
                                                op0=ALU.mult, op1=ALU.add))
            pick(left[:], second[:])
            link(nc.vector.tensor_tensor(first[:], first[:], second[:], ALU.add))
            link(nc.vector.tensor_tensor(weight[:].rearrange("p (t e) -> p t e", e=EXPERTS), prob[:], first[:],
                                         ALU.mult))
            dve.wait_ge(wqk_hi_ready, 1)
            nc.vector.tensor_tensor(wqk_split[:, :, :, 1, :], wqkv[:, :, 0:2, :],
                                    wqk_split[:, :, :, 0, :].bitcast(F32), ALU.subtract).then_inc(wqk_lo_ready, 1)
            dve.wait_ge(ffn_zero, 1)

            def add_y(e, tb):
                s = e * BATCH + tb
                dve.wait_ge(y_ready, s + 1)
                for t in range(BT):
                    tile = tb * BT + t
                    at = tile * EXPERTS + e
                    w = weight[:, at:at + 1] if isinstance(e, int) else weight[:, bass.ds(at, 1)]
                    nc.vector.scalar_tensor_tensor(out=ffn[:, tile, :], in0=y_bank[tb % 2][:, t * D:(t + 1) * D],
                                                   scalar=w, in1=ffn[:, tile, :], op0=ALU.mult, op1=ALU.add)\
                        .then_inc(ffn_added, 1)

            def expert(e, slot, half):
                for tb in range(BATCH):
                    for c in range(NC):
                        n = e * (BATCH * NC) + tb * NC + c
                        if c == 0:
                            s = e * BATCH + tb
                            if not isinstance(s, int) or s >= 2:
                                dve.wait_ge(y_ready, s - 1)
                        m = CHUNKS[c]
                        k = (tb * NC + c) % 2
                        dve.wait_ge(up_ready, n + 1)
                        dve.wait_ge(silu_ready, n + 1)
                        nc.vector.tensor_tensor(hidden[0:m, tb % 2, c, :], up_bank[k][0:m, :], gate_act[0:m, k, :],
                                                ALU.mult).then_inc(hidden_ready, 1)
                    if tb == 0:
                        if not is_first(e):
                            add_y(e - 1, BATCH - 1)
                    else:
                        add_y(e, tb - 1)
                    if tb == 1 and not is_last(e, EXPERTS):
                        split_lo(e + 1, 1 - slot)

            over_experts(dve, expert)
            add_y(EXPERTS - 1, BATCH - 1)

            def copy_lo(u, ready_hi, hi, lo, lo_ready, b):
                dve.wait_ge(ready_hi, u + 1)
                nc.vector.tensor_tensor(lo[:], misc[b][:], hi[:].bitcast(F32), ALU.subtract).then_inc(lo_ready, 1)

            def maxima(u, kind, half_of_tiles):
                h = 2 * u + kind
                its = slice(2 * half_of_tiles, 2 * half_of_tiles + 2)
                dve.wait_ge(scores_ready, BT * h + 2 * half_of_tiles + 2)
                nc.vector.reduce_max(row_max[:, kind, its], score[:, its, :], AX_X).then_inc(max_ready, 1)
                dve.wait_ge(max_ready, 2 * h + half_of_tiles + 1)
                nc.vector.tensor_scalar(exp_bias[:, kind, its], row_max[:, kind, its], -SCALE, None, ALU.mult)\
                    .then_inc(bias_ready, 1)

            def inverse(u, kind, half_of_tiles):
                h = 2 * u + kind
                its = slice(2 * half_of_tiles, 2 * half_of_tiles + 2)
                dve.wait_ge(exp_ready, BT * h + 2 * half_of_tiles + 2)
                nc.vector.reciprocal(inv_sum[:, kind, its], exp_sum[:, kind, its]).then_inc(inv_ready, 1)

            def copy_v(u, slot, b):
                dve.wait_ge(v_ready, u + 1)
                nc.vector.tensor_copy(v_unit[:, slot].rearrange("p t c -> p (t c)"), misc[b][:]).then_inc(v_copied, 1)

            def copy_probsT(u, kind, jt):
                h = 2 * u + kind
                if jt == 1 and not is_first(u):
                    dve.wait_ge(attn_ready, u)
                dve.wait_ge(probsT_ready, BT * h + jt + 1)
                nc.vector.tensor_copy(probsT[:, kind, jt, :], tr_bank[1][:]).then_inc(copied_by_dve, 1)

            def add_proj(u, b):
                dve.wait_ge(proj_ready, u + 1)
                z = group(xn, u // PAIRS)
                nc.vector.tensor_tensor(z, misc[b][:].rearrange("p (t d) -> p t d", d=D), z, ALU.add)\
                    .then_inc(proj_added, 1)

            copy_lo(0, q_hi_ready, q_hi, q_lo, q_lo_ready, Q_BANK[0])
            copy_lo(0, k_hi_ready, k_hi, k_lo, k_lo_ready, K_BANK[0])
            copy_v(0, 0, V_BANK[0])
            maxima(0, A, 0)
            maxima(0, A, 1)
            inverse(0, A, 0)
            inverse(0, A, 1)

            def unit(u, slot, half):
                more = not is_last(u, UNITS)
                nxt = 1 - slot
                if more:
                    copy_lo(u + 1, q_hi_ready, q_hi, q_lo, q_lo_ready, Q_BANK[nxt])
                maxima(u, B, 0)
                if more:
                    copy_lo(u + 1, k_hi_ready, k_hi, k_lo, k_lo_ready, K_BANK[nxt])
                maxima(u, B, 1)
                if not is_first(u):
                    add_proj(u - 1, PROJ_BANK[slot])
                copy_probsT(u, A, 1)
                inverse(u, B, 0)
                copy_probsT(u, A, 3)
                inverse(u, B, 1)
                if more:
                    copy_v(u + 1, nxt, V_BANK[nxt])
                    maxima(u + 1, A, 0)
                    maxima(u + 1, A, 1)
                copy_probsT(u, B, 1)
                copy_probsT(u, B, 3)
                if more:
                    inverse(u + 1, A, 0)
                    inverse(u + 1, A, 1)

            over_units(dve, unit)
            add_proj(UNITS - 1, PROJ_BANK[0])

            dve.wait_ge(const_loaded, 32)
            dve.wait_ge(ffn_ready, GROUPS)
            dve.wait_ge(proj_added, UNITS)
            STEPS = 9
            with dve.Fori(0, GROUPS) as g:
                base = STEPS * g
                layer_norm(g, xn, xn, fin_var_ready, fin_rstd_ready, fin_step, base)
                z, s = group(xn, g), group(scratch, g)
                nc.vector.tensor_tensor(z, z, spread(cols(rstd, g, BT), D), ALU.mult).then_inc(fin_step, 1)
                dve.wait_ge(fin_step, base + 6)
                nc.vector.tensor_tensor(z, z, gamma[:].unsqueeze(1).to_broadcast([P, BT, D]), ALU.mult)\
                    .then_inc(fin_step, 1)
                dve.wait_ge(fin_step, base + 7)
                nc.vector.tensor_tensor(z, z, beta[:].unsqueeze(1).to_broadcast([P, BT, D]), ALU.add)\
                    .then_inc(fin_step, 1)
                dve.wait_ge(fin_step, base + 8)
                nc.vector.tensor_tensor(z, z, group(ffn, g), ALU.mult).then_inc(fin_step, 1)
                dve.wait_ge(fin_step, base + 9)
                nc.vector.tensor_tensor(s, z, group(x, g), ALU.add).then_inc(fin_ready, 1)

        @block.tensor
        def _(pe):
            def split_matmul(dst, w_hi, w_lo, m_hi, m_lo):
                nc.tensor.matmul(dst, w_hi, m_hi, start=True, stop=False)
                nc.tensor.matmul(dst, w_hi, m_lo, start=False, stop=False)
                return nc.tensor.matmul(dst, w_lo, m_hi, start=False, stop=True)

            pe.wait_ge(ident_ready, 1)
            for g in range(GROUPS):
                pe.wait_ge(xn_ready, g + 1)
                for t in range(BT):
                    last = nc.tensor.transpose(score[:, g, t * P:(t + 1) * P], xn[:, g * BT + t, :], ident[:])
                last.then_inc(xnT_ready, 1)
            pe.wait_ge(router_loaded, 16)
            pe.wait_ge(xnT_f32_ready, GROUPS)
            for t in range(TILES):
                last = nc.tensor.matmul(bank[0][:, t * EXPERTS:(t + 1) * EXPERTS], xnT[:, t * P:(t + 1) * P],
                                        router[:], start=True, stop=True)
            last.then_inc(logits_ready, 1)

            def gate_up(e, slot, tb):
                x_hi, x_lo = xnT_hi[:, tb * SEQ:(tb + 1) * SEQ], xnT_lo[:, tb * SEQ:(tb + 1) * SEQ]
                if tb == 0:
                    pe.wait_ge(gu_lo_ready, e + 1)
                    if is_first(e):
                        pe.wait_ge(xnT_lo_ready, GROUPS)
                for c in range(NC):
                    n = e * (BATCH * NC) + tb * NC + c
                    k = (tb * NC + c) % 2
                    m = CHUNKS[c]
                    if not isinstance(n, int) or n >= 2:
                        pe.wait_ge(hidden_ready, n - 1)
                    for part, dst, ready in ((0, gate_bank[k], gate_ready), (1, up_bank[k], up_ready)):
                        at = part * INTER + c * P
                        split_matmul(dst[0:m, :], gu_hi[:, slot, at:at + m], gu_lo[:, slot, at:at + m], x_hi, x_lo)\
                            .then_inc(ready, 1)

            def down_products(e, slot, half, tb):
                s = e * BATCH + tb
                pe.wait_ge(hidden_ready, NC * (s + 1))
                if tb == 0:
                    pe.wait_ge(down_loaded[slot], 16 * NC * (half + 1))
                if is_first(e) and tb == 0:
                    pe.wait_ge(shifted_ready, 1)
                if not isinstance(s, int) or s >= 2:
                    pe.wait_ge(ffn_added, BT * (s - 1))
                for t in range(BT):
                    for c in range(NC):
                        m = CHUNKS[c]
                        last = nc.tensor.matmul(y_bank[tb % 2][:, t * D:(t + 1) * D],
                                                hidden[0:m, tb % 2, c, t * P:(t + 1) * P], down[0:m, slot, c, :],
                                                start=c == 0, stop=c == NC - 1)
                last.then_inc(y_ready, 1)

            def expert(e, slot, half):
                for tb in range(1, BATCH):
                    gate_up(e, slot, tb)
                    down_products(e, slot, half, tb - 1)
                if not is_last(e, EXPERTS):
                    gate_up(e + 1, 1 - slot, 0)
                down_products(e, slot, half, BATCH - 1)

            gate_up(0, 0, 0)
            over_experts(pe, expert)

            def project(u, slot, half, part, b, ready):
                if part == 0:
                    pe.wait_ge(unit_loaded[slot], 32 * (half + 1))
                bt = u // PAIRS
                w = w_unit[:, slot, part]
                split_matmul(misc[b][:], w[:, 0, :], w[:, 1, :], cols(xnT_hi, bt, SEQ), cols(xnT_lo, bt, SEQ))\
                    .then_inc(ready, 1)

            def project_v(u, slot, b):
                pair = u % PAIRS
                w = wqkv[:, pair, 2, :] if isinstance(u, int) else \
                    wqkv[:, bass.ds(pair, 1), 2, :].rearrange("p o c -> p (o c)")
                for jt in range(BT):
                    last = nc.tensor.matmul(misc[b][:, jt * P:(jt + 1) * P], x_unit[:, slot, jt * P:(jt + 1) * P], w,
                                            start=True, stop=True)
                last.then_inc(v_ready, 1)

            def scores(u, kind, slot, half, its):
                h = 2 * u + kind
                if kind == A and its[0] == 0:
                    pe.wait_ge(stack_loaded[slot], 16 * STACK_DMAS * (half + 1))
                for it in its:
                    if not isinstance(h, int) or h >= 1:
                        pe.wait_ge(exp_ready, BT * (h - 1) + it + 1)
                    q = q_stack[:, slot, kind, it * P:(it + 1) * P]
                    nc.tensor.matmul(score[:, it, :], q, k_hi_stack[:, slot, kind, :], start=True, stop=False)
                    nc.tensor.matmul(score[:, it, :], q, k_lo_stack[:, slot, kind, :], start=False, stop=True)\
                        .then_inc(scores_ready, 1)

            def transposes(u, kind):
                h = 2 * u + kind
                for jt in range(BT):
                    copied, n = ((copied_by_act, copied_by_dve)[jt % 2], 2 * h + jt // 2)
                    if not isinstance(n, int) or n >= 1:
                        pe.wait_ge(copied, n)
                    for it in range(BT):
                        if jt == 0:
                            pe.wait_ge(probs_ready, BT * h + it + 1)
                        last = nc.tensor.transpose(tr_bank[jt % 2][:, it * P:(it + 1) * P],
                                                   probs[:, kind, it, jt * P:(jt + 1) * P], ident[:])
                    last.then_inc(probsT_ready, 1)

            def attend(u, slot, b):
                pe.wait_ge(v_copied, u + 1)
                for jt in range(BT):
                    copied, n = ((copied_by_act, copied_by_dve)[jt % 2], 4 * u + 2 + jt // 2 + 1)
                    pe.wait_ge(copied, n)
                    for kind in (A, B):
                        last = nc.tensor.matmul(misc[b][kind * DH:(kind + 1) * DH, :],
                                                v_unit[:, slot, jt, kind * DH:(kind + 1) * DH],
                                                probsT[:, kind, jt, :], start=jt == 0, stop=jt == BT - 1)
                last.then_inc(attn_ready, 1)

            def out_project(u, b):
                pe.wait_ge(attn_copied, u + 1)
                pair = u % PAIRS
                w = wo[:, pair, :] if isinstance(u, int) else \
                    wo[:, bass.ds(pair, 1), :].rearrange("p o c -> p (o c)")
                for it in range(BT):
                    last = nc.tensor.matmul(misc[b][:, it * D:(it + 1) * D], attnT[:, it * P:(it + 1) * P], w,
                                            start=True, stop=True)
                last.then_inc(proj_ready, 1)

            pe.wait_ge(ffn_added, EXPERTS * TILES)
            pe.wait_ge(attn_w_loaded, 32)
            project(0, 0, 0, 0, Q_BANK[0], q_ready)
            project(0, 0, 0, 1, K_BANK[0], k_ready)
            pe.wait_ge(k_lo_ready, 1)
            project_v(0, 0, V_BANK[0])
            scores(0, A, 0, 0, range(BT))

            def unit(u, slot, half):
                more = not is_last(u, UNITS)
                nxt, nhalf = 1 - slot, half + slot
                if more:
                    pe.wait_ge(v_copied, u + 1)
                    project(u + 1, nxt, nhalf, 0, Q_BANK[nxt], q_ready)
                scores(u, B, slot, half, (0, 1))
                if more:
                    if is_first(u):
                        pe.wait_ge(q_lo_ready, 1)
                    else:
                        pe.wait_ge(attn_copied, u)
                    project(u + 1, nxt, nhalf, 1, K_BANK[nxt], k_ready)
                scores(u, B, slot, half, (2, 3))
                if not is_first(u):
                    if more:
                        pe.wait_ge(q_lo_ready, u + 2)
                    else:
                        pe.wait_ge(v_copied, u + 1)
                    out_project(u - 1, PROJ_BANK[slot])
                transposes(u, A)
                if more:
                    pe.wait_ge(k_lo_ready, u + 2)
                    project_v(u + 1, nxt, V_BANK[nxt])
                    scores(u + 1, A, nxt, nhalf, range(BT))
                transposes(u, B)
                if is_first(u):
                    pe.wait_ge(q_lo_ready, 2)
                else:
                    pe.wait_ge(proj_added, u)
                attend(u, slot, PV_BANK[slot])

            over_units(pe, unit)
            out_project(UNITS - 1, PROJ_BANK[0])


Q_BANK = [1, 0]
K_BANK = [0, 1]
V_BANK = [0, 1]
PROJ_BANK = [0, 1]
PV_BANK = [0, 1]
STACK_DMAS = 12


def kernel(L0_attn_h, L0_attn_Wq, L0_attn_Wk, L0_attn_Wv, L0_attn_Wo, L0_attn_gamma, L0_attn_beta,
           L0_ffn_router_w, L0_ffn_gate_w, L0_ffn_up_w, L0_ffn_down_w):
    import numpy as np
    import concourse.bacc as bacc
    from concourse.bass_utils import run_bass_kernel_spmd

    def tiles(a):
        return np.asarray(a).reshape(TILES, P, D).transpose(1, 0, 2)

    def pairs(w):
        return np.asarray(w).reshape(D, PAIRS, P)

    arrays = {
        "x_in": tiles(L0_attn_h),
        "wqkv_in": np.stack([pairs(L0_attn_Wq), pairs(L0_attn_Wk), pairs(L0_attn_Wv)], axis=2),
        "wo_in": np.asarray(L0_attn_Wo).reshape(PAIRS, P, D).transpose(1, 0, 2),
        "gamma_in": np.asarray(L0_attn_gamma),
        "beta_in": np.asarray(L0_attn_beta),
        "router_in": np.asarray(L0_ffn_router_w).T,
        "gate_up_in": np.concatenate([np.asarray(L0_ffn_gate_w), np.asarray(L0_ffn_up_w)], axis=1).transpose(0, 2, 1),
        "down_in": np.asarray(L0_ffn_down_w).transpose(0, 2, 1).reshape(EXPERTS * INTER, D),
    }
    arrays = {name: np.ascontiguousarray(a) for name, a in arrays.items()}
    nc = bacc.Bacc("TRN2", target_bir_lowering=False, num_devices=1)
    args = [nc.dram_tensor(name, a.shape, mybir.dt.from_np(a.dtype), kind="ExternalInput").ap()
            for name, a in arrays.items()]
    out = nc.dram_tensor("out", (P, TILES, D), F32, kind="ExternalOutput").ap()
    program(nc, *args, out)
    result = run_bass_kernel_spmd(nc, [arrays], core_ids=[0])
    y = result.results[0]["out"]
    return y.transpose(1, 0, 2).reshape(BATCH, SEQ, D)
```

```python
from contextlib import ExitStack

import concourse.bass as bass
from concourse import mybir

F32 = mybir.dt.float32
F32R = mybir.dt.float32r
ALU = mybir.AluOpType
ACT = mybir.ActivationFunctionType
AX_X = mybir.AxisListType.X

P = 128
D = 128
BATCH, SEQ = 4, 512
TOKENS = BATCH * SEQ
TILES = TOKENS // P
BT = SEQ // P
GROUPS = TILES // BT
HEADS, DH = 16, 64
PAIRS = HEADS // 2
UNITS = BATCH * PAIRS
SCALE = 1.0 / DH ** 0.5
LN_EPS = 1e-5
EXPERTS, INTER = 8, 352
STEPS = 4
CHUNKS = [128, 128, 96]
NC = len(CHUNKS)
A, B = 0, 1


def program(nc, x_in, wqkv_in, wo_in, gamma_in, beta_in, router_in, gate_up_in, down_in, out):
    ctx = ExitStack()
    with ctx:
        def sb(name, shape, dt=F32):
            return ctx.enter_context(nc.sbuf_tensor(name, shape, dt))

        def sem(name):
            return ctx.enter_context(nc.semaphore(name))

        x = sb("x", [P, TILES, D])
        xn = sb("xn", [P, TILES, D])
        scratch = sb("scratch", [P, TILES, D])
        ffn = sb("ffn", [P, TILES, D])
        xnT = sb("xnT", [D, TOKENS])
        xnT_hi = sb("xnT_hi", [D, TOKENS], F32R)
        xnT_lo = sb("xnT_lo", [D, TOKENS], F32R)
        ident = sb("ident", [P, P])
        gamma = sb("gamma", [P, D])
        beta = sb("beta", [P, D])
        row_sum = sb("row_sum", [P, TILES])
        mean = sb("mean", [P, TILES])
        sq_sum = sb("sq_sum", [P, TILES])
        var_eps = sb("var_eps", [P, TILES])
        rstd = sb("rstd", [P, TILES])
        minus_half = sb("minus_half", [P, TILES])
        router = sb("router", [D, EXPERTS])
        rank = sb("rank", [P, TILES, EXPERTS])
        prob = sb("prob", [P, TILES, EXPERTS])
        left = sb("left", [P, TILES, EXPERTS])
        eq = sb("eq", [P, TILES, EXPERTS])
        first = sb("first", [P, TILES, EXPERTS])
        second = sb("second", [P, TILES, EXPERTS])
        weight = sb("weight", [P, TILES * EXPERTS])
        best = sb("best", [P, TILES])
        gu_hi = sb("gu_hi", [D, 2, 2 * INTER], F32R)
        gu_lo = sb("gu_lo", [D, 2, 2 * INTER], F32R)
        down = sb("down", [P, 2, NC, D])
        wqkv = sb("wqkv", [D, PAIRS, 3, P])
        wqk_split = sb("wqk_split", [D, PAIRS, 2, 2, P], F32R)
        wo = sb("wo", [P, PAIRS, D])
        w_unit = sb("w_unit", [D, 2, 2, 2, P], F32R)
        x_unit = sb("x_unit", [D, 2, SEQ])
        q_hi = sb("q_hi", [P, SEQ], F32R)
        q_lo = sb("q_lo", [P, SEQ], F32R)
        k_hi = sb("k_hi", [P, SEQ], F32R)
        k_lo = sb("k_lo", [P, SEQ], F32R)
        q_stack = sb("q_stack", [P, 2, 2, SEQ], F32R)
        k_hi_stack = sb("k_hi_stack", [P, 2, 2, SEQ], F32R)
        k_lo_stack = sb("k_lo_stack", [P, 2, 2, SEQ], F32R)
        v_unit = sb("v_unit", [P, 2, BT, P])
        row_max = sb("row_max", [P, 2, BT])
        exp_bias = sb("exp_bias", [P, 2, BT])
        exp_sum = sb("exp_sum", [P, 2, BT])
        inv_sum = sb("inv_sum", [P, 2, BT])
        probs = sb("probs", [P, 2, BT, SEQ])
        late = sb("late", [P, 2 * 2 * BT * SEQ])
        probsT = late[:].rearrange("p (s h j i) -> p s h j i", s=2, h=2, j=BT)
        hidden = late[:, 0:2 * NC * SEQ].rearrange("p (s c t) -> p s c t", s=2, c=NC)
        gate_act = late[:, 2 * NC * SEQ:(2 * NC + 2) * SEQ].rearrange("p (s t) -> p s t", s=2)
        gu_raw = late[:, (2 * NC + 2) * SEQ:(2 * NC + 2) * SEQ + 4 * INTER].rearrange("p (s n) -> p s n", s=2)
        attnT = sb("attnT", [P, SEQ])

        bank = [ctx.enter_context(nc.psum_tensor(f"bank{i}", [P, SEQ], F32)) for i in range(3)]
        score = ctx.enter_context(nc.psum_tensor("score", [P, BT, SEQ], F32))
        extra = ctx.enter_context(nc.psum_tensor("extra", [P, SEQ], F32))
        misc = [bank[0], bank[1]]
        tr_bank = [bank[2], extra]
        gate_bank = [score[:, 0, :], score[:, 1, :]]
        up_bank = [score[:, 2, :], score[:, 3, :]]
        y_bank = [bank[0], bank[1]]

        x_loaded = [sem(f"x_loaded{g}") for g in range(GROUPS)]
        router_loaded, const_loaded, attn_w_loaded = sem("router_loaded"), sem("const_loaded"), sem("attn_w_loaded")
        gu_loaded = [sem("gu_loaded0"), sem("gu_loaded1")]
        down_loaded = [sem("down_loaded0"), sem("down_loaded1")]
        ident_zero, ident_ready, consts_ready = sem("ident_zero"), sem("ident_ready"), sem("consts_ready")
        stat_step, var_ready, rstd_ready, xn_ready = sem("stat_step"), sem("var_ready"), sem("rstd_ready"), sem("xn_ready")
        xnT_ready, xnT_hi_ready, xnT_f32_ready, xnT_lo_ready = sem("xnT_ready"), sem("xnT_hi_ready"), sem("xnT_f32_ready"), sem("xnT_lo_ready")
        logits_ready, shifted_ready, router_exp_ready, route_step = sem("logits_ready"), sem("shifted_ready"), sem("router_exp_ready"), sem("route_step")
        wqk_hi_ready, wqk_lo_ready = sem("wqk_hi_ready"), sem("wqk_lo_ready")
        gu_hi_ready, gu_lo_ready = sem("gu_hi_ready"), sem("gu_lo_ready")
        gate_ready, up_ready, silu_ready, hidden_ready = sem("gate_ready"), sem("up_ready"), sem("silu_ready"), sem("hidden_ready")
        y_ready, ffn_zero, ffn_added, ffn_ready = sem("y_ready"), sem("ffn_zero"), sem("ffn_added"), sem("ffn_ready")
        unit_loaded = [sem("unit_loaded0"), sem("unit_loaded1")]
        stack_loaded = [sem("stack_loaded0"), sem("stack_loaded1")]
        q_ready, k_ready, v_ready = sem("q_ready"), sem("k_ready"), sem("v_ready")
        q_hi_ready, q_lo_ready, k_hi_ready, k_lo_ready, v_copied = (
            sem("q_hi_ready"), sem("q_lo_ready"), sem("k_hi_ready"), sem("k_lo_ready"), sem("v_copied"))
        scores_ready, max_ready, bias_ready, exp_ready = sem("scores_ready"), sem("max_ready"), sem("bias_ready"), sem("exp_ready")
        inv_ready, probs_ready = sem("inv_ready"), sem("probs_ready")
        probsT_ready, copied_by_act, copied_by_dve = sem("probsT_ready"), sem("copied_by_act"), sem("copied_by_dve")
        attn_ready, attn_copied, proj_ready, proj_added = sem("attn_ready"), sem("attn_copied"), sem("proj_ready"), sem("proj_added")
        fin_step, fin_var_ready, fin_rstd_ready, fin_ready = sem("fin_step"), sem("fin_var_ready"), sem("fin_rstd_ready"), sem("fin_ready")
        pool_turn = sem("pool_turn")
        stored = sem("stored")

        def group(t, g):
            return t[:, bass.ds(g * BT, BT), :] if not isinstance(g, int) else t[:, g * BT:(g + 1) * BT, :]

        def cols(t, g, n):
            return t[:, bass.ds(g * n, n)] if not isinstance(g, int) else t[:, g * n:(g + 1) * n]

        def spread(t, n):
            return t.unsqueeze(2).to_broadcast([t.shape[0], t.shape[1], n])

        block = ctx.enter_context(nc.Block())

        def over_units(eng, body):
            body(0, 0, 0)
            body(1, 1, 0)
            with eng.Fori(1, UNITS // 2 - 1) as i:
                body(2 * i, 0, i)
                body(2 * i + 1, 1, i)
            body(UNITS - 2, 0, UNITS // 2 - 1)
            body(UNITS - 1, 1, UNITS // 2 - 1)

        def over_experts(eng, body):
            body(0, 0, 0)
            with eng.Fori(0, EXPERTS // 2 - 1) as i:
                body(2 * i + 1, 1, i)
                body(2 * i + 2, 0, i + 1)
            body(EXPERTS - 1, 1, EXPERTS // 2 - 1)

        def is_first(u):
            return isinstance(u, int) and u == 0

        def from_unit(u, n):
            return not isinstance(u, int) or u >= n

        def is_last(u, n):
            return isinstance(u, int) and u == n - 1

        @block.sync
        def _(sp):
            for g in range(GROUPS):
                sp.dma_start(group(x, g), group(x_in, g)).then_inc(x_loaded[g], 16)
            sp.dma_start(router[:], router_in).then_inc(router_loaded, 16)

            def load_expert(e, slot):
                sp.dma_start(gu_raw[:, slot, :], gu_dram(e)).then_inc(gu_loaded[slot], 16)
                for c in range(NC):
                    sp.dma_start(down[0:CHUNKS[c], slot, c, :], down_dram(e, c)).then_inc(down_loaded[slot], 16)

            def gu_dram(e):
                return gate_up_in[bass.ds(e, 1), :, :].rearrange("e p n -> (e p) n") if not isinstance(e, int) else gate_up_in[e, :, :]

            def down_dram(e, c):
                return down_in[bass.ds(e * INTER + c * P, CHUNKS[c]), :] if not isinstance(e, int) else \
                    down_in[e * INTER + c * P:e * INTER + c * P + CHUNKS[c], :]

            load_expert(0, 0)
            load_expert(1, 1)
            sp.dma_start(wqkv[:], wqkv_in).then_inc(attn_w_loaded, 16)
            sp.dma_start(wo[:], wo_in).then_inc(attn_w_loaded, 16)
            sp.dma_start(gamma[:], gamma_in.partition_broadcast(P)).then_inc(const_loaded, 16)
            sp.dma_start(beta[:], beta_in.partition_broadcast(P)).then_inc(const_loaded, 16)
            with sp.Fori(0, EXPERTS // 2 - 1) as i:
                for slot in range(2):
                    e = 2 * i + 2 + slot
                    sp.wait_ge(y_ready, BATCH * (e - 1))
                    load_expert(e, slot)

            def load_unit(u, slot):
                b, pair = u // PAIRS, u % PAIRS
                if isinstance(u, int):
                    w_src, x_src = wqk_split[:, pair], xnT[:, b * SEQ:(b + 1) * SEQ]
                else:
                    w_src = wqk_split[:, bass.ds(pair, 1)].rearrange("p o a s c -> p (o a) s c")
                    x_src = xnT[:, bass.ds(b * SEQ, SEQ)]
                if not isinstance(u, int) or u >= 2:
                    sp.wait_ge(v_ready, u - 1)
                sp.dma_start(w_unit[:, slot].bitcast(F32), w_src.bitcast(F32)).then_inc(unit_loaded[slot], 16)
                sp.dma_start(x_unit[:, slot, :], x_src).then_inc(unit_loaded[slot], 16)

            def stack_unit(u, slot):
                for ready, src, stacks in ((q_hi_ready, q_hi, [q_stack[0:DH, slot]]),
                                           (q_lo_ready, q_lo, [q_stack[DH:P, slot]]),
                                           (k_hi_ready, k_hi, [k_hi_stack[0:DH, slot], k_hi_stack[DH:P, slot]]),
                                           (k_lo_ready, k_lo, [k_lo_stack[0:DH, slot], k_lo_stack[DH:P, slot]])):
                    sp.wait_ge(ready, u + 1)
                    for dst in stacks:
                        for h in (A, B):
                            sp.dma_start(dst[:, h, :].bitcast(F32), src[h * DH:(h + 1) * DH, :].bitcast(F32)).then_inc(stack_loaded[slot], 16)

            sp.wait_ge(wqk_lo_ready, 1)
            sp.wait_ge(xnT_f32_ready, GROUPS)
            load_unit(0, 0)
            load_unit(1, 1)
            stack_unit(0, 0)

            stack_unit(1, 1)
            with sp.Fori(0, UNITS // 2 - 1) as i:
                load_unit(2 * i + 2, 0)
                stack_unit(2 * i + 2, 0)
                load_unit(2 * i + 3, 1)
                stack_unit(2 * i + 3, 1)

            with sp.Fori(0, GROUPS) as g:
                sp.wait_ge(fin_ready, g + 1)
                sp.dma_start(group(out, g), group(scratch, g)).then_inc(stored, 16)
            sp.wait_ge(stored, 16 * GROUPS)

        @block.gpsimd
        def _(pool):
            nc.gpsimd.memset(ident[:], 0.0).then_inc(ident_zero, 1)
            nc.gpsimd.memset(minus_half[:], -0.5).then_inc(consts_ready, 1)
            pool.wait_ge(ident_zero, 1)
            nc.gpsimd.affine_select(out=ident[:], in_=ident[:], compare_op=ALU.not_equal, fill=1.0,
                                    base=0, pattern=[[-1, P]], channel_multiplier=1).then_inc(ident_ready, 1)
            pool.wait_ge(consts_ready, 1)
            with pool.Fori(0, GROUPS) as g:
                pool.wait_ge(var_ready, g + 1)
                nc.gpsimd.tensor_tensor(cols(rstd, g, BT), cols(var_eps, g, BT), cols(minus_half, g, BT),
                                        ALU.pow).then_inc(rstd_ready, 1)
            for e in range(EXPERTS):
                nc.gpsimd.memset(rank[:, :, e], float(EXPERTS - e)).then_inc(consts_ready, 1)
            nc.gpsimd.memset(ffn[:], 0.0).then_inc(ffn_zero, 1)

            def normalise(n, kind, half):
                pool.wait_ge(inv_ready, n + 1)
                pool.sem_inc(pool_turn, 1)
                for it in (2 * half, 2 * half + 1):
                    nc.gpsimd.tensor_scalar(probs[:, kind, it, :], probs[:, kind, it, :],
                                            inv_sum[:, kind, it:it + 1], 1.0, ALU.mult, ALU.mult)\
                        .then_inc(probs_ready, 1)

            with pool.Fori(0, UNITS) as u:
                for k in range(STEPS):
                    normalise(STEPS * u + k, k // 2, k % 2)

            with pool.Fori(0, GROUPS) as g:
                pool.wait_ge(fin_var_ready, g + 1)
                nc.gpsimd.tensor_tensor(cols(rstd, g, BT), cols(var_eps, g, BT), cols(minus_half, g, BT),
                                        ALU.pow).then_inc(fin_rstd_ready, 1)

        @block.scalar
        def _(act):
            for g in range(GROUPS):
                act.wait_ge(xnT_ready, g + 1)
                nc.scalar.activation(cols(xnT_hi, g, SEQ), score[:, g, :], ACT.Copy).then_inc(xnT_hi_ready, 1)
                nc.scalar.activation(cols(xnT, g, SEQ), score[:, g, :], ACT.Copy).then_inc(xnT_f32_ready, 1)
            act.wait_ge(shifted_ready, 1)
            nc.scalar.activation(prob[:], left[:], ACT.Exp).then_inc(router_exp_ready, 1)

            def split_hi(e, slot):
                act.wait_ge(gu_loaded[slot], 16 * ((e // 2) + 1))
                if not isinstance(e, int) or e >= 2:
                    act.wait_ge(y_ready, BATCH * (e - 1))
                nc.scalar.activation(gu_hi[:, slot, :], gu_raw[:, slot, :], ACT.Copy).then_inc(gu_hi_ready, 1)

            split_hi(0, 0)
            act.wait_ge(attn_w_loaded, 32)
            nc.scalar.activation(wqk_split[:, :, :, 0, :], wqkv[:, :, 0:2, :], ACT.Copy).then_inc(wqk_hi_ready, 1)

            def expert(e, slot, half):
                for tb in range(BATCH):
                    for c in range(NC):
                        n = e * (BATCH * NC) + tb * NC + c
                        ln = n if isinstance(n, int) else None
                        act.wait_ge(gate_ready, n + 1)
                        if ln is None or ln >= 2:
                            act.wait_ge(hidden_ready, n - 1)
                        m = CHUNKS[c]
                        k = (tb * NC + c) % 2
                        nc.scalar.activation(gate_act[0:m, k, :], gate_bank[k][0:m, :], ACT.Silu)\
                            .then_inc(silu_ready, 1)
                    if tb == 1 and not is_last(e, EXPERTS):
                        split_hi(e + 1, 1 - slot)

            over_experts(act, expert)

            with act.Fori(0, GROUPS) as g:
                act.wait_ge(ffn_added, TILES * (EXPERTS - 1) + BT * (g + 1))
                nc.scalar.activation(group(ffn, g), group(ffn, g), ACT.Silu).then_inc(ffn_ready, 1)

            def copy_hi(u, ready, b, hi, hi_ready):
                act.wait_ge(ready, u + 1)
                nc.scalar.activation(hi[:], misc[b][:], ACT.Copy).then_inc(hi_ready, 1)

            def exps(n, kind, half):
                act.wait_ge(bias_ready, n + 1)
                if from_unit(n, STEPS):
                    act.wait_ge(probsT_ready, 2 * (n - STEPS + 1))
                for it in (2 * half, 2 * half + 1):
                    nc.scalar.activation(probs[:, kind, it, :], score[:, it, :], ACT.Exp,
                                         bias=exp_bias[:, kind, it:it + 1], scale=SCALE,
                                         accum_out=exp_sum[:, kind, it:it + 1]).then_inc(exp_ready, 1)

            def copy_probsT(n, u, slot, kind, half):
                if kind == A and half == 0 and from_unit(u, 2):
                    act.wait_ge(attn_ready, u - 1)
                it = 2 * half
                act.wait_ge(probsT_ready, 2 * n + 1)
                nc.scalar.activation(probsT[:, slot, kind, :, it * P:(it + 1) * P],
                                     tr_bank[0][:].rearrange("p (j i) -> p j i", i=P), ACT.Copy)\
                    .then_inc(copied_by_act, 1)

            def copy_attn(u, slot):
                act.wait_ge(attn_ready, u + 1)
                nc.scalar.activation(attnT[:], misc[PV_BANK[slot]][:], ACT.Copy).then_inc(attn_copied, 1)

            copy_hi(0, q_ready, Q_BANK[0], q_hi, q_hi_ready)
            copy_hi(0, k_ready, K_BANK[0], k_hi, k_hi_ready)

            def unit(u, slot, turn):
                nxt, n = 1 - slot, STEPS * u
                if from_unit(u, 2):
                    copy_attn(u - 2, slot)
                if from_unit(u, 1):
                    copy_probsT(n - 2, u - 1, nxt, B, 0)
                exps(n, A, 0)
                if not is_last(u, UNITS):
                    act.wait_ge(stack_loaded[slot], 16 * STACK_DMAS * (turn + 1))
                    copy_hi(u + 1, q_ready, Q_BANK[nxt], q_hi, q_hi_ready)
                    copy_hi(u + 1, k_ready, K_BANK[nxt], k_hi, k_hi_ready)
                if from_unit(u, 1):
                    copy_probsT(n - 1, u - 1, nxt, B, 1)
                exps(n + 1, A, 1)
                copy_probsT(n, u, slot, A, 0)
                exps(n + 2, B, 0)
                copy_probsT(n + 1, u, slot, A, 1)
                exps(n + 3, B, 1)

            over_units(act, unit)
            copy_attn(UNITS - 2, 0)
            copy_probsT(STEPS * UNITS - 2, UNITS - 1, 1, B, 0)
            copy_probsT(STEPS * UNITS - 1, UNITS - 1, 1, B, 1)
            copy_attn(UNITS - 1, 1)

        @block.vector
        def _(dve):
            def layer_norm(g, src, dst, var_sem, rstd_sem, step_sem, base):
                nc.vector.reduce_sum(cols(row_sum, g, BT), group(src, g), AX_X).then_inc(step_sem, 1)
                dve.wait_ge(step_sem, base + 1)
                nc.vector.tensor_scalar(cols(mean, g, BT), cols(row_sum, g, BT), 1.0 / D, None, ALU.mult)\
                    .then_inc(step_sem, 1)
                dve.wait_ge(step_sem, base + 2)
                nc.vector.tensor_tensor(group(dst, g), group(src, g), spread(cols(mean, g, BT), D),
                                        ALU.subtract).then_inc(step_sem, 1)
                dve.wait_ge(step_sem, base + 3)
                nc.vector.tensor_tensor(group(scratch, g), group(dst, g), group(dst, g), ALU.mult)\
                    .then_inc(step_sem, 1)
                dve.wait_ge(step_sem, base + 4)
                nc.vector.reduce_sum(cols(sq_sum, g, BT), group(scratch, g), AX_X).then_inc(step_sem, 1)
                dve.wait_ge(step_sem, base + 5)
                nc.vector.tensor_scalar(cols(var_eps, g, BT), cols(sq_sum, g, BT), 1.0 / D, LN_EPS,
                                        ALU.mult, ALU.add).then_inc(var_sem, 1)
                dve.wait_ge(rstd_sem, g + 1)

            for g in range(GROUPS):
                dve.wait_ge(x_loaded[g], 16)
                layer_norm(g, x, xn, var_ready, rstd_ready, stat_step, 5 * g)
                nc.vector.tensor_tensor(group(xn, g), group(xn, g), spread(cols(rstd, g, BT), D), ALU.mult)\
                    .then_inc(xn_ready, 1)
            for g in range(GROUPS):
                dve.wait_ge(xnT_f32_ready, g + 1)
                nc.vector.tensor_tensor(cols(xnT_lo, g, SEQ), score[:, g, :], cols(xnT_hi, g, SEQ).bitcast(F32),
                                        ALU.subtract).then_inc(xnT_lo_ready, 1)

            def split_lo(e, slot):
                dve.wait_ge(gu_hi_ready, e + 1)
                nc.vector.tensor_tensor(gu_lo[:, slot, :], gu_raw[:, slot, :], gu_hi[:, slot, :].bitcast(F32),
                                        ALU.subtract).then_inc(gu_lo_ready, 1)

            step = [0]

            def link(instruction):
                step[0] += 1
                instruction.then_inc(route_step, 1)
                dve.wait_ge(route_step, step[0])

            lg = bank[0][:, 0:TILES * EXPERTS].rearrange("p (t e) -> p t e", e=EXPERTS)
            dve.wait_ge(logits_ready, 1)
            link(nc.vector.reduce_max(best[:], lg, AX_X))
            nc.vector.tensor_tensor(left[:], lg, spread(best[:], EXPERTS), ALU.subtract).then_inc(shifted_ready, 1)
            dve.wait_ge(router_exp_ready, 1)
            split_lo(0, 0)
            link(nc.vector.reduce_sum(best[:], prob[:], AX_X))
            link(nc.vector.reciprocal(best[:], best[:]))
            link(nc.vector.tensor_tensor(prob[:], prob[:], spread(best[:], EXPERTS), ALU.mult))
            dve.wait_ge(consts_ready, 1 + EXPERTS)

            def pick(values, chosen):
                link(nc.vector.reduce_max(best[:], values, AX_X))
                link(nc.vector.tensor_tensor(eq[:], values, spread(best[:], EXPERTS), ALU.is_equal))
                link(nc.vector.tensor_tensor(eq[:], eq[:], rank[:], ALU.mult))
                link(nc.vector.reduce_max(best[:], eq[:], AX_X))
                link(nc.vector.tensor_tensor(chosen, eq[:], spread(best[:], EXPERTS), ALU.is_equal))

            pick(prob[:], first[:])
            link(nc.vector.scalar_tensor_tensor(out=left[:], in0=first[:], scalar=-2.0, in1=prob[:],
                                                op0=ALU.mult, op1=ALU.add))
            pick(left[:], second[:])
            link(nc.vector.tensor_tensor(first[:], first[:], second[:], ALU.add))
            link(nc.vector.tensor_tensor(weight[:].rearrange("p (t e) -> p t e", e=EXPERTS), prob[:], first[:],
                                         ALU.mult))
            dve.wait_ge(wqk_hi_ready, 1)
            nc.vector.tensor_tensor(wqk_split[:, :, :, 1, :], wqkv[:, :, 0:2, :],
                                    wqk_split[:, :, :, 0, :].bitcast(F32), ALU.subtract).then_inc(wqk_lo_ready, 1)
            dve.wait_ge(ffn_zero, 1)

            def add_y(e, tb):
                s = e * BATCH + tb
                dve.wait_ge(y_ready, s + 1)
                for t in range(BT):
                    tile = tb * BT + t
                    at = tile * EXPERTS + e
                    w = weight[:, at:at + 1] if isinstance(e, int) else weight[:, bass.ds(at, 1)]
                    nc.vector.scalar_tensor_tensor(out=ffn[:, tile, :], in0=y_bank[tb % 2][:, t * D:(t + 1) * D],
                                                   scalar=w, in1=ffn[:, tile, :], op0=ALU.mult, op1=ALU.add)\
                        .then_inc(ffn_added, 1)

            def expert(e, slot, half):
                for tb in range(BATCH):
                    for c in range(NC):
                        n = e * (BATCH * NC) + tb * NC + c
                        if c == 0:
                            s = e * BATCH + tb
                            if not isinstance(s, int) or s >= 2:
                                dve.wait_ge(y_ready, s - 1)
                        m = CHUNKS[c]
                        k = (tb * NC + c) % 2
                        dve.wait_ge(up_ready, n + 1)
                        dve.wait_ge(silu_ready, n + 1)
                        nc.vector.tensor_tensor(hidden[0:m, tb % 2, c, :], up_bank[k][0:m, :], gate_act[0:m, k, :],
                                                ALU.mult).then_inc(hidden_ready, 1)
                    if tb == 0:
                        if not is_first(e):
                            add_y(e - 1, BATCH - 1)
                    else:
                        add_y(e, tb - 1)
                    if tb == 1 and not is_last(e, EXPERTS):
                        split_lo(e + 1, 1 - slot)

            over_experts(dve, expert)
            add_y(EXPERTS - 1, BATCH - 1)

            def copy_lo(u, ready_hi, hi, lo, lo_ready, b):
                dve.wait_ge(ready_hi, u + 1)
                nc.vector.tensor_tensor(lo[:], misc[b][:], hi[:].bitcast(F32), ALU.subtract).then_inc(lo_ready, 1)

            def maxima(n, kind, half):
                its = slice(2 * half, 2 * half + 2)
                dve.wait_ge(scores_ready, 2 * (n + 1))
                nc.vector.reduce_max(row_max[:, kind, its], score[:, its, :], AX_X).then_inc(max_ready, 1)
                dve.wait_ge(max_ready, n + 1)
                nc.vector.tensor_scalar(exp_bias[:, kind, its], row_max[:, kind, its], -SCALE, None, ALU.mult)\
                    .then_inc(bias_ready, 1)

            def inverse(n, kind, half):
                its = slice(2 * half, 2 * half + 2)
                dve.wait_ge(exp_ready, 2 * (n + 1))
                nc.vector.reciprocal(inv_sum[:, kind, its], exp_sum[:, kind, its]).then_inc(inv_ready, 1)

            def copy_v(u, slot):
                dve.wait_ge(v_ready, u + 1)
                nc.vector.tensor_copy(v_unit[:, slot].rearrange("p t c -> p (t c)"), misc[V_BANK[slot]][:])\
                    .then_inc(v_copied, 1)

            def copy_probsT(n, u, slot, kind, half):
                if kind == A and half == 0 and from_unit(u, 2):
                    dve.wait_ge(attn_ready, u - 1)
                it = 2 * half + 1
                dve.wait_ge(probsT_ready, 2 * n + 2)
                nc.vector.tensor_copy(probsT[:, slot, kind, :, it * P:(it + 1) * P],
                                      tr_bank[1][:].rearrange("p (j i) -> p j i", i=P)).then_inc(copied_by_dve, 1)

            def add_proj(u, slot):
                dve.wait_ge(proj_ready, u + 1)
                z = group(xn, u // PAIRS)
                nc.vector.tensor_tensor(z, misc[PROJ_BANK[slot]][:].rearrange("p (t d) -> p t d", d=D), z, ALU.add)\
                    .then_inc(proj_added, 1)

            copy_lo(0, q_hi_ready, q_hi, q_lo, q_lo_ready, Q_BANK[0])
            copy_lo(0, k_hi_ready, k_hi, k_lo, k_lo_ready, K_BANK[0])

            def unit(u, slot, turn):
                nxt, n = 1 - slot, STEPS * u
                if from_unit(u, 1):
                    inverse(n - 1, B, 1)
                maxima(n, A, 0)
                if from_unit(u, 1):
                    copy_probsT(n - 2, u - 1, nxt, B, 0)
                if not is_last(u, UNITS):
                    copy_lo(u + 1, q_hi_ready, q_hi, q_lo, q_lo_ready, Q_BANK[nxt])
                    copy_lo(u + 1, k_hi_ready, k_hi, k_lo, k_lo_ready, K_BANK[nxt])
                inverse(n, A, 0)
                maxima(n + 1, A, 1)
                if from_unit(u, 1):
                    copy_probsT(n - 1, u - 1, nxt, B, 1)
                copy_v(u, slot)
                if from_unit(u, 2):
                    add_proj(u - 2, slot)
                inverse(n + 1, A, 1)
                maxima(n + 2, B, 0)
                copy_probsT(n, u, slot, A, 0)
                inverse(n + 2, B, 0)
                maxima(n + 3, B, 1)
                copy_probsT(n + 1, u, slot, A, 1)

            over_units(dve, unit)
            inverse(STEPS * UNITS - 1, B, 1)
            copy_probsT(STEPS * UNITS - 2, UNITS - 1, 1, B, 0)
            copy_probsT(STEPS * UNITS - 1, UNITS - 1, 1, B, 1)
            add_proj(UNITS - 2, 0)
            dve.wait_ge(proj_added, UNITS - 1)
            add_proj(UNITS - 1, 1)

            dve.wait_ge(const_loaded, 32)
            dve.wait_ge(ffn_ready, GROUPS)
            dve.wait_ge(proj_added, UNITS)
            FIN_STEPS = 9
            with dve.Fori(0, GROUPS) as g:
                base = FIN_STEPS * g
                layer_norm(g, xn, xn, fin_var_ready, fin_rstd_ready, fin_step, base)
                z, s = group(xn, g), group(scratch, g)
                nc.vector.tensor_tensor(z, z, spread(cols(rstd, g, BT), D), ALU.mult).then_inc(fin_step, 1)
                dve.wait_ge(fin_step, base + 6)
                nc.vector.tensor_tensor(z, z, gamma[:].unsqueeze(1).to_broadcast([P, BT, D]), ALU.mult)\
                    .then_inc(fin_step, 1)
                dve.wait_ge(fin_step, base + 7)
                nc.vector.tensor_tensor(z, z, beta[:].unsqueeze(1).to_broadcast([P, BT, D]), ALU.add)\
                    .then_inc(fin_step, 1)
                dve.wait_ge(fin_step, base + 8)
                nc.vector.tensor_tensor(z, z, group(ffn, g), ALU.mult).then_inc(fin_step, 1)
                dve.wait_ge(fin_step, base + 9)
                nc.vector.tensor_tensor(s, z, group(x, g), ALU.add).then_inc(fin_ready, 1)

        @block.tensor
        def _(pe):
            def split_matmul(dst, w_hi, w_lo, m_hi, m_lo):
                nc.tensor.matmul(dst, w_hi, m_hi, start=True, stop=False)
                nc.tensor.matmul(dst, w_hi, m_lo, start=False, stop=False)
                return nc.tensor.matmul(dst, w_lo, m_hi, start=False, stop=True)

            pe.wait_ge(ident_ready, 1)
            for g in range(GROUPS):
                pe.wait_ge(xn_ready, g + 1)
                for t in range(BT):
                    last = nc.tensor.transpose(score[:, g, t * P:(t + 1) * P], xn[:, g * BT + t, :], ident[:])
                last.then_inc(xnT_ready, 1)
            pe.wait_ge(router_loaded, 16)
            pe.wait_ge(xnT_f32_ready, GROUPS)
            for t in range(TILES):
                last = nc.tensor.matmul(bank[0][:, t * EXPERTS:(t + 1) * EXPERTS], xnT[:, t * P:(t + 1) * P],
                                        router[:], start=True, stop=True)
            last.then_inc(logits_ready, 1)

            def gate_up(e, slot, tb):
                x_hi, x_lo = xnT_hi[:, tb * SEQ:(tb + 1) * SEQ], xnT_lo[:, tb * SEQ:(tb + 1) * SEQ]
                if tb == 0:
                    pe.wait_ge(gu_lo_ready, e + 1)
                    if is_first(e):
                        pe.wait_ge(xnT_lo_ready, GROUPS)
                for c in range(NC):
                    n = e * (BATCH * NC) + tb * NC + c
                    k = (tb * NC + c) % 2
                    m = CHUNKS[c]
                    if not isinstance(n, int) or n >= 2:
                        pe.wait_ge(hidden_ready, n - 1)
                    for part, dst, ready in ((0, gate_bank[k], gate_ready), (1, up_bank[k], up_ready)):
                        at = part * INTER + c * P
                        split_matmul(dst[0:m, :], gu_hi[:, slot, at:at + m], gu_lo[:, slot, at:at + m], x_hi, x_lo)\
                            .then_inc(ready, 1)

            def down_products(e, slot, half, tb):
                s = e * BATCH + tb
                pe.wait_ge(hidden_ready, NC * (s + 1))
                if tb == 0:
                    pe.wait_ge(down_loaded[slot], 16 * NC * (half + 1))
                if is_first(e) and tb == 0:
                    pe.wait_ge(shifted_ready, 1)
                if not isinstance(s, int) or s >= 2:
                    pe.wait_ge(ffn_added, BT * (s - 1))
                for t in range(BT):
                    for c in range(NC):
                        m = CHUNKS[c]
                        last = nc.tensor.matmul(y_bank[tb % 2][:, t * D:(t + 1) * D],
                                                hidden[0:m, tb % 2, c, t * P:(t + 1) * P], down[0:m, slot, c, :],
                                                start=c == 0, stop=c == NC - 1)
                last.then_inc(y_ready, 1)

            def expert(e, slot, half):
                for tb in range(1, BATCH):
                    gate_up(e, slot, tb)
                    down_products(e, slot, half, tb - 1)
                if not is_last(e, EXPERTS):
                    gate_up(e + 1, 1 - slot, 0)
                down_products(e, slot, half, BATCH - 1)

            gate_up(0, 0, 0)
            over_experts(pe, expert)

            def project(u, slot, turn, part, b, ready):
                if part == 0:
                    pe.wait_ge(unit_loaded[slot], 32 * (turn + 1))
                bt = u // PAIRS
                w = w_unit[:, slot, part]
                split_matmul(misc[b][:], w[:, 0, :], w[:, 1, :], cols(xnT_hi, bt, SEQ), cols(xnT_lo, bt, SEQ))\
                    .then_inc(ready, 1)

            def project_v(u, slot, b):
                pair = u % PAIRS
                w = wqkv[:, pair, 2, :] if isinstance(u, int) else \
                    wqkv[:, bass.ds(pair, 1), 2, :].rearrange("p o c -> p (o c)")
                for jt in range(BT):
                    last = nc.tensor.matmul(misc[b][:, jt * P:(jt + 1) * P], x_unit[:, slot, jt * P:(jt + 1) * P], w,
                                            start=True, stop=True)
                last.then_inc(v_ready, 1)

            def scores(n, kind, half, slot, turn):
                if kind == A and half == 0:
                    pe.wait_ge(stack_loaded[slot], 16 * STACK_DMAS * (turn + 1))
                if from_unit(n, 2):
                    pe.wait_ge(exp_ready, 2 * (n - 1))
                for it in (2 * half, 2 * half + 1):
                    q = q_stack[:, slot, kind, it * P:(it + 1) * P]
                    nc.tensor.matmul(score[:, it, :], q, k_hi_stack[:, slot, kind, :], start=True, stop=False)
                    nc.tensor.matmul(score[:, it, :], q, k_lo_stack[:, slot, kind, :], start=False, stop=True)\
                        .then_inc(scores_ready, 1)

            def transposes(n, kind, half):
                for j, copied in ((0, copied_by_act), (1, copied_by_dve)):
                    it = 2 * half + j
                    pe.wait_ge(probs_ready, 2 * n + j + 1)
                    if from_unit(n, 1):
                        pe.wait_ge(copied, n)
                    for jt in range(BT):
                        last = nc.tensor.transpose(tr_bank[j][:, jt * P:(jt + 1) * P],
                                                   probs[:, kind, it, jt * P:(jt + 1) * P], ident[:])
                    last.then_inc(probsT_ready, 1)

            def attend(u, slot, key_tiles):
                if key_tiles[0] == 0:
                    pe.wait_ge(v_copied, u + 1)
                    pe.wait_ge(copied_by_act, STEPS * (u + 1))
                    pe.wait_ge(copied_by_dve, STEPS * (u + 1))
                for jt in key_tiles:
                    for kind in (A, B):
                        last = nc.tensor.matmul(misc[PV_BANK[slot]][kind * DH:(kind + 1) * DH, :],
                                                v_unit[:, slot, jt, kind * DH:(kind + 1) * DH],
                                                probsT[:, slot, kind, jt, :], start=jt == 0, stop=jt == BT - 1)
                if key_tiles[-1] == BT - 1:
                    last.then_inc(attn_ready, 1)

            def out_project(u, b):
                pe.wait_ge(attn_copied, u + 1)
                pair = u % PAIRS
                w = wo[:, pair, :] if isinstance(u, int) else \
                    wo[:, bass.ds(pair, 1), :].rearrange("p o c -> p (o c)")
                for it in range(BT):
                    last = nc.tensor.matmul(misc[b][:, it * D:(it + 1) * D], attnT[:, it * P:(it + 1) * P], w,
                                            start=True, stop=True)
                last.then_inc(proj_ready, 1)

            pe.wait_ge(ffn_added, EXPERTS * TILES)
            pe.wait_ge(attn_w_loaded, 32)
            project(0, 0, 0, 0, Q_BANK[0], q_ready)
            project(0, 0, 0, 1, K_BANK[0], k_ready)

            def unit(u, slot, turn):
                more = not is_last(u, UNITS)
                nxt, n = 1 - slot, STEPS * u
                scores(n, A, 0, slot, turn)
                if from_unit(u, 1):
                    transposes(n - 2, B, 0)
                if more:
                    if is_first(u):
                        pe.wait_ge(k_lo_ready, 1)
                    project(u + 1, nxt, turn + slot, 0, Q_BANK[nxt], q_ready)
                    if from_unit(u, 2):
                        pe.wait_ge(attn_copied, u - 1)
                    else:
                        pe.wait_ge(*((v_copied, 1) if u else (q_lo_ready, 1)))
                    project(u + 1, nxt, turn + slot, 1, K_BANK[nxt], k_ready)
                scores(n + 1, A, 1, slot, turn)
                if from_unit(u, 1):
                    transposes(n - 1, B, 1)
                if more:
                    pe.wait_ge(q_lo_ready, u + 2)
                else:
                    pe.wait_ge(proj_added, u - 2)
                project_v(u, slot, V_BANK[slot])
                if from_unit(u, 2):
                    if more:
                        pe.wait_ge(k_lo_ready, u + 2)
                    out_project(u - 2, PROJ_BANK[slot])
                scores(n + 2, B, 0, slot, turn)
                transposes(n, A, 0)
                if from_unit(u, 1):
                    pe.wait_ge(v_copied, u + 1)
                    attend(u - 1, nxt, (0, 1))
                scores(n + 3, B, 1, slot, turn)
                transposes(n + 1, A, 1)
                if from_unit(u, 1):
                    attend(u - 1, nxt, (2, 3))

            over_units(pe, unit)
            transposes(STEPS * UNITS - 2, B, 0)
            transposes(STEPS * UNITS - 1, B, 1)
            out_project(UNITS - 2, PROJ_BANK[0])
            pe.wait_ge(proj_added, UNITS - 2)
            attend(UNITS - 1, 1, range(BT))
            out_project(UNITS - 1, PROJ_BANK[1])


Q_BANK = [1, 0]
K_BANK = [0, 1]
V_BANK = [0, 1]
PROJ_BANK = [1, 0]
PV_BANK = [1, 0]
STACK_DMAS = 12


def kernel(L0_attn_h, L0_attn_Wq, L0_attn_Wk, L0_attn_Wv, L0_attn_Wo, L0_attn_gamma, L0_attn_beta,
           L0_ffn_router_w, L0_ffn_gate_w, L0_ffn_up_w, L0_ffn_down_w):
    import numpy as np
    import concourse.bacc as bacc
    from concourse.bass_utils import run_bass_kernel_spmd

    def tiles(a):
        return np.asarray(a).reshape(TILES, P, D).transpose(1, 0, 2)

    def pairs(w):
        return np.asarray(w).reshape(D, PAIRS, P)

    arrays = {
        "x_in": tiles(L0_attn_h),
        "wqkv_in": np.stack([pairs(L0_attn_Wq), pairs(L0_attn_Wk), pairs(L0_attn_Wv)], axis=2),
        "wo_in": np.asarray(L0_attn_Wo).reshape(PAIRS, P, D).transpose(1, 0, 2),
        "gamma_in": np.asarray(L0_attn_gamma),
        "beta_in": np.asarray(L0_attn_beta),
        "router_in": np.asarray(L0_ffn_router_w).T,
        "gate_up_in": np.concatenate([np.asarray(L0_ffn_gate_w), np.asarray(L0_ffn_up_w)], axis=1).transpose(0, 2, 1),
        "down_in": np.asarray(L0_ffn_down_w).transpose(0, 2, 1).reshape(EXPERTS * INTER, D),
    }
    arrays = {name: np.ascontiguousarray(a) for name, a in arrays.items()}
    nc = bacc.Bacc("TRN2", target_bir_lowering=False, num_devices=1)
    args = [nc.dram_tensor(name, a.shape, mybir.dt.from_np(a.dtype), kind="ExternalInput").ap()
            for name, a in arrays.items()]
    out = nc.dram_tensor("out", (P, TILES, D), F32, kind="ExternalOutput").ap()
    program(nc, *args, out)
    result = run_bass_kernel_spmd(nc, [arrays], core_ids=[0])
    y = result.results[0]["out"]
    return y.transpose(1, 0, 2).reshape(BATCH, SEQ, D)
```

```python
from contextlib import ExitStack

import concourse.bass as bass
from concourse import mybir

F32 = mybir.dt.float32
F32R = mybir.dt.float32r
I32, U32 = mybir.dt.int32, mybir.dt.uint32
ALU = mybir.AluOpType
ACT = mybir.ActivationFunctionType
AX_X = mybir.AxisListType.X

P = 128
D = 128
BATCH, SEQ = 4, 512
TOKENS = BATCH * SEQ
TILES = TOKENS // P
BT = SEQ // P
GROUPS = TILES // BT
HEADS, DH = 16, 64
PAIRS = HEADS // 2
UNITS = BATCH * PAIRS
SCALE = 1.0 / DH ** 0.5
LN_EPS = 1e-5
EXPERTS, INTER = 8, 352
SPLITS = [slice(0, 2), slice(2, PAIRS)]
STEPS = 4
CHOICES = 2
PICKS = CHOICES * TOKENS
SLOTS = (PICKS + (P - 1) * EXPERTS) // P
RING = 4
RINGS = -(-SLOTS // RING)
ROW = D + 2
CHUNKS = [128, 128, 96]
NC = len(CHUNKS)
A, B = 0, 1


def program(nc, x_in, wqkv_in, wo_in, gamma_in, beta_in, router_in, gate_up_in, down_in, out):
    ctx = ExitStack()
    with ctx:
        def sb(name, shape, dt=F32):
            return ctx.enter_context(nc.sbuf_tensor(name, shape, dt))

        def sem(name):
            return ctx.enter_context(nc.semaphore(name))

        x = sb("x", [P, TILES, D])
        xn = sb("xn", [P, TILES, D])
        z = sb("z", [P, TILES, D])
        xnT_hi = sb("xnT_hi", [D, TOKENS], F32R)
        xnT_lo = sb("xnT_lo", [D, TOKENS], F32R)
        tokens_t = sb("tokens_t", [D, TOKENS + 2 * SEQ])
        xnT = tokens_t[:, 0:TOKENS]
        x_unit = tokens_t[:, TOKENS:].rearrange("p (s t) -> p s t", s=2)
        ident = sb("ident", [P, P])
        gamma = sb("gamma", [P, D])
        beta = sb("beta", [P, D])
        stats = sb("stats", [P, BT, 6])
        first_mean_var = sb("first_mean_var", [P, GROUPS, BT, 2])
        first_rstd = sb("first_rstd", [P, TILES])
        mean_var = sb("mean_var", [P, BT, 2])
        var_eps = sb("var_eps", [P, BT])
        rstd = sb("rstd", [P, BT])
        minus_half = sb("minus_half", [P, BT])
        router = sb("router", [D, EXPERTS])
        rank = sb("rank", [P, TILES, EXPERTS])
        prob = sb("prob", [P, TILES, EXPERTS])
        left = sb("left", [P, TILES, EXPERTS])
        eq = sb("eq", [P, TILES, EXPERTS])
        best = sb("best", [P, TILES])
        chosen = sb("chosen", [P, CHOICES, TILES, EXPERTS])
        before = sb("before", [P, P])
        ones = sb("ones", [P, P])
        running = sb("running", [P, 2, TILES, EXPERTS])
        both = sb("both", [P, TILES, EXPERTS])
        order_int = sb("order_int", [P, TILES + SLOTS], I32)
        order = sb("order", [P, TILES + SLOTS])
        above = sb("above", [P, SLOTS, EXPERTS])
        ends = sb("ends", [P, 2, EXPERTS])
        tiles_of = sb("tiles_of", [P, EXPERTS])
        counted = sb("counted", [P, (TILES + 1) * EXPERTS])
        place = sb("place", [P, TILES, EXPERTS])
        position = sb("position", [P, TILES, CHOICES])
        position_int = sb("position_int", [P, TILES * CHOICES], U32)
        expert_of = sb("expert_of", [P, SLOTS])
        expert_int = sb("expert_int", [P, SLOTS], I32)
        meta = sb("meta", [P, TILES, CHOICES, 2])
        staged = sb("staged", [P, ROW])
        staged_position = sb("staged_position", [P, 1], U32)
        down = sb("down", [P, EXPERTS, NC, D])
        down_flat = down[:].rearrange("p e c d -> p (e c d)")
        rows = sb("rows", [P, RING, ROW])
        rows_meta = sb("rows_meta", [P, SLOTS, 2])
        rows_index = sb("rows_index", [P, 4], U32)
        rows_t = sb("rows_t", [P, 2, P])
        hidden_t = sb("hidden_t", [P, 2, NC, P])
        result = sb("result", [P, 4, D])
        wqkv = sb("wqkv", [D, PAIRS, 3, P])
        wqk_split = sb("wqk_split", [D, PAIRS, 2, 2, P], F32R)
        wo = sb("wo", [P, PAIRS, D])
        wo_flat = wo[:].rearrange("p a d -> p (a d)")
        w_unit = sb("w_unit", [D, 2, 2, 2, P], F32R)
        q_hi = sb("q_hi", [P, SEQ], F32R)
        q_lo = sb("q_lo", [P, SEQ], F32R)
        k_hi = sb("k_hi", [P, SEQ], F32R)
        k_lo = sb("k_lo", [P, SEQ], F32R)
        q_stack = sb("q_stack", [P, 2, 2, SEQ], F32R)
        k_hi_stack = sb("k_hi_stack", [P, 2, 2, SEQ], F32R)
        k_lo_stack = sb("k_lo_stack", [P, 2, 2, SEQ], F32R)
        v_unit = sb("v_unit", [P, 2, BT, P])
        row_max = sb("row_max", [P, 2, BT])
        exp_bias = sb("exp_bias", [P, 2, BT])
        exp_sum = sb("exp_sum", [P, 2, BT])
        inv_sum = sb("inv_sum", [P, 2, BT])
        probs = sb("probs", [P, 2, BT, SEQ])
        gate_act = probs[:, A, 0:2, 0:INTER]
        hidden = probs[:, B, 0:2, 0:INTER]
        wqkv_flat = wqkv[:].rearrange("p a b c -> p (a b c)")
        gate_w = wqkv_flat[:, 0:EXPERTS * INTER]
        up_w = tokens_t[:, 0:EXPERTS * INTER]
        late = sb("late", [P, 2 * 2 * BT * SEQ])
        probsT = late[:].rearrange("p (s h j i) -> p s h j i", s=2, h=2, j=BT)
        picked = late[:, 0:TILES * CHOICES * D].rearrange("p (t k d) -> p t k d", k=CHOICES, d=D)
        attnT = sb("attnT", [P, SEQ])

        bank = [ctx.enter_context(nc.psum_tensor(f"bank{i}", [P, SEQ], F32)) for i in range(3)]
        score = ctx.enter_context(nc.psum_tensor("score", [P, BT, SEQ], F32))
        extra = ctx.enter_context(nc.psum_tensor("extra", [P, SEQ], F32))
        misc = [bank[0], bank[1]]
        tr_bank = [bank[2], extra]
        logits_bank = bank[2]
        gate_bank = [score[:, 0, :], score[:, 1, :]]
        up_bank = [score[:, 2, :], score[:, 3, :]]
        rows_bank, hidden_bank = bank[1], bank[0]
        result_bank = [bank[2], extra]

        sorted_rows = nc.dram_tensor("sorted_rows", [RINGS * RING * P, ROW], F32).ap()
        results = nc.dram_tensor("results", [PICKS + RING * P, D], F32).ap()

        x_loaded = [sem(f"x_loaded{g}") for g in range(GROUPS)]
        router_loaded, const_loaded, wo_loaded = sem("router_loaded"), sem("const_loaded"), sem("wo_loaded")
        wqkv_loaded = [sem("wqkv_loaded0"), sem("wqkv_loaded1")]
        gate_up_loaded, down_loaded = sem("gate_up_loaded"), sem("down_loaded")
        rows_loaded = [sem(f"rows_loaded{s}") for s in range(4)]
        returned = [sem(f"returned{s}") for s in range(4)]
        picked_loaded = [sem(f"picked_loaded{g}") for g in range(GROUPS)]
        ident_zero, ident_ready, consts_ready = sem("ident_zero"), sem("ident_ready"), sem("consts_ready")
        stat_step, var_ready, rstd_ready, xn_ready = sem("stat_step"), sem("var_ready"), sem("rstd_ready"), sem("xn_ready")
        xnT_ready, xnT_f32_ready, xnT_lo_ready = sem("xnT_ready"), sem("xnT_f32_ready"), sem("xnT_lo_ready")
        logits_ready, shifted_ready, router_exp_ready, route_step = sem("logits_ready"), sem("shifted_ready"), sem("router_exp_ready"), sem("route_step")
        wqk_hi_ready, wqk_lo_ready = sem("wqk_hi_ready"), sem("wqk_lo_ready")
        order_consts, order_float, running_ready, order_counted, order_read = (
            sem("order_consts"), sem("order_float"), sem("running_ready"), sem("order_counted"), sem("order_read"))
        positions_ready, experts_ready = sem("positions_ready"), sem("experts_ready")
        blank_step, blank_ready, blank_moved, scattered, staged_ready = sem("blank_step"), sem("blank_ready"), sem("blank_moved"), sem("scattered"), sem("staged_ready")
        rows_t_ready, rows_t_copied = sem("rows_t_ready"), sem("rows_t_copied")
        gate_ready, up_ready, silu_ready, hidden_ready = sem("gate_ready"), sem("up_ready"), sem("silu_ready"), sem("hidden_ready")
        hidden_t_ready, hidden_t_copied = sem("hidden_t_ready"), sem("hidden_t_copied")
        product_ready, result_ready, index_ready = sem("product_ready"), sem("result_ready"), sem("index_ready")
        z_copied, summed_ready, gate_silu_ready = sem("z_copied"), sem("summed_ready"), sem("gate_silu_ready")
        unit_loaded = [sem("unit_loaded0"), sem("unit_loaded1")]
        stack_loaded = [[sem(f"stack_loaded{slot}{kind}") for kind in "AB"] for slot in range(2)]
        q_ready, k_ready, v_ready = sem("q_ready"), sem("k_ready"), sem("v_ready")
        q_hi_ready, q_lo_ready, k_hi_ready, k_lo_ready, v_copied = (
            sem("q_hi_ready"), sem("q_lo_ready"), sem("k_hi_ready"), sem("k_lo_ready"), sem("v_copied"))
        scores_ready, max_ready, bias_ready, exp_ready = sem("scores_ready"), sem("max_ready"), sem("bias_ready"), sem("exp_ready")
        inv_ready, probs_ready = sem("inv_ready"), sem("probs_ready")
        probsT_ready, copied_by_act, copied_by_dve = sem("probsT_ready"), sem("copied_by_act"), sem("copied_by_dve")
        attn_ready, attn_copied, proj_ready, proj_added = sem("attn_ready"), sem("attn_copied"), sem("proj_ready"), sem("proj_added")
        fin_step, fin_var_ready, fin_rstd_ready, fin_ready = sem("fin_step"), sem("fin_var_ready"), sem("fin_rstd_ready"), sem("fin_ready")
        tail_step, last_fin_ready = sem("tail_step"), sem("last_fin_ready")
        pool_turn, dve_turn = sem("pool_turn"), sem("dve_turn")
        stored = sem("stored")

        def group(t, g):
            return t[:, bass.ds(g * BT, BT), :] if not isinstance(g, int) else t[:, g * BT:(g + 1) * BT, :]

        def cols(t, g, n):
            return t[:, bass.ds(g * n, n)] if not isinstance(g, int) else t[:, g * n:(g + 1) * n]

        def columns(t, at, n):
            return t[:, bass.ds(at, n)] if not isinstance(at, int) else t[:, at:at + n]

        def spread(t, n):
            return t.unsqueeze(2).to_broadcast([t.shape[0], t.shape[1], n])

        block = ctx.enter_context(nc.Block())

        def over_units(eng, body):
            body(0, 0, 0)
            body(1, 1, 0)
            with eng.Fori(1, UNITS // 2 - 1) as i:
                body(2 * i, 0, i)
                body(2 * i + 1, 1, i)
            body(UNITS - 2, 0, UNITS // 2 - 1)
            body(UNITS - 1, 1, UNITS // 2 - 1)

        def over_tiles(eng, body):
            for s in range(4):
                body(s, s, 0)
            turns = (SLOTS - 4) // 8
            with eng.Fori(0, turns) as turn:
                for s in range(8):
                    body(8 * turn + 4 + s, s % 4, 2 * turn + 1 + s // 4)
            first = 4 + 8 * turns
            for i in range(first, SLOTS):
                body(i, i % 4, i // 4)

        def is_first(u):
            return isinstance(u, int) and u == 0

        def from_unit(u, n):
            return not isinstance(u, int) or u >= n

        def is_last(u, n):
            return isinstance(u, int) and u == n - 1

        @block.sync
        def _(sp):
            for g in range(GROUPS):
                sp.dma_start(group(x, g), group(x_in, g)).then_inc(x_loaded[g], 16)
            for part, pairs in enumerate(SPLITS):
                sp.dma_start(wqkv[:, pairs], wqkv_in[:, pairs]).then_inc(wqkv_loaded[part], 16)
                if part == 0:
                    sp.dma_start(router[:], router_in).then_inc(router_loaded, 16)

            def load_unit(u, slot):
                b, pair = u // PAIRS, u % PAIRS
                if isinstance(u, int):
                    w_src, x_src = wqk_split[:, pair], xnT[:, b * SEQ:(b + 1) * SEQ]
                else:
                    w_src = wqk_split[:, bass.ds(pair, 1)].rearrange("p o a s c -> p (o a) s c")
                    x_src = xnT[:, bass.ds(b * SEQ, SEQ)]
                if not isinstance(u, int) or u >= 2:
                    sp.wait_ge(v_ready, u - 1)
                sp.dma_start(w_unit[:, slot].bitcast(F32), w_src.bitcast(F32)).then_inc(unit_loaded[slot], 16)
                sp.dma_start(x_unit[:, slot, :], x_src).then_inc(unit_loaded[slot], 16)

            def stack_unit(u, slot):
                for heads in (((A,), (B,)) if is_first(u) else ((A, B),)):
                    for ready, src, stacks in ((q_hi_ready, q_hi, [q_stack[0:DH, slot]]),
                                               (q_lo_ready, q_lo, [q_stack[DH:P, slot]]),
                                               (k_hi_ready, k_hi, [k_hi_stack[0:DH, slot], k_hi_stack[DH:P, slot]]),
                                               (k_lo_ready, k_lo, [k_lo_stack[0:DH, slot], k_lo_stack[DH:P, slot]])):
                        if A in heads:
                            sp.wait_ge(ready, u + 1)
                        for dst in stacks:
                            for h in heads:
                                sp.dma_start(dst[:, h, :].bitcast(F32), src[h * DH:(h + 1) * DH, :].bitcast(F32))\
                                    .then_inc(stack_loaded[slot][h], 16)

            sp.wait_ge(wqk_lo_ready, 1)
            sp.wait_ge(xnT_f32_ready, 1)
            load_unit(0, 0)
            load_unit(1, 1)
            stack_unit(0, 0)
            sp.wait_ge(blank_ready, 1)
            by_slot = sorted_rows.rearrange("(j s p) c -> p s j c", p=P, s=RING)
            for s in range(RING):
                sp.dma_start(by_slot[:, s], rows[:, s:s + 1, :].to_broadcast([P, RINGS, ROW])).then_inc(blank_moved, 16)
            stack_unit(1, 1)
            sp.dma_start(wo[:], wo_in).then_inc(wo_loaded, 16)
            sp.wait_ge(wqk_lo_ready, len(SPLITS))
            sp.wait_ge(xnT_f32_ready, GROUPS)
            with sp.Fori(0, UNITS // 2 - 1) as i:
                load_unit(2 * i + 2, 0)
                stack_unit(2 * i + 2, 0)
                load_unit(2 * i + 3, 1)
                stack_unit(2 * i + 3, 1)

            for c in range(NC):
                sp.dma_start(down[0:CHUNKS[c], :, c, :], down_in.rearrange("(e i) d -> i e d", e=EXPERTS)
                             [c * P:c * P + CHUNKS[c], :, :]).then_inc(down_loaded, 16)
            sp.dma_start(gamma[:], gamma_in.partition_broadcast(P)).then_inc(const_loaded, 16)
            sp.dma_start(beta[:], beta_in.partition_broadcast(P)).then_inc(const_loaded, 16)
            sp.wait_ge(v_ready, UNITS)
            for part, w in ((0, gate_w), (1, up_w)):
                sp.dma_start(w.rearrange("p (e n) -> p e n", e=EXPERTS),
                             gate_up_in.rearrange("e p n -> p e n")[:, :, part * INTER:(part + 1) * INTER])\
                    .then_inc(gate_up_loaded, 16)
            sp.wait_ge(scattered, 16 * (PICKS // P))

            def load_rows(i, s, j):
                if from_unit(i, 4):
                    sp.wait_ge(rows_t_copied, i - 3)
                src = sorted_rows[i * P:(i + 1) * P, :] if isinstance(i, int) else sorted_rows[bass.ds(i * P, P), :]
                sp.dma_start(rows[:, s, :], src).then_inc(rows_loaded[s], 16)

            over_tiles(sp, load_rows)
            for s in range(4):
                sp.wait_ge(returned[s], 16 * ((SLOTS - s + 3) // 4))
            by_token = results[0:PICKS, :].rearrange("(t p k) d -> p t k d", p=P, k=CHOICES)
            for g in range(GROUPS):
                sp.dma_start(picked[:, g * BT:(g + 1) * BT], by_token[:, g * BT:(g + 1) * BT]).then_inc(picked_loaded[g], 16)
            for g in range(GROUPS):
                sp.wait_ge(*((fin_ready, g + 1) if g < GROUPS - 1 else (last_fin_ready, 1)))
                sp.dma_start(group(out, g), group(z, g)).then_inc(stored, 16)
            sp.wait_ge(stored, 16 * GROUPS)

        @block.gpsimd
        def _(pool):
            nc.gpsimd.memset(minus_half[:], -0.5).then_inc(consts_ready, 1)
            nc.gpsimd.memset(ident[:], 0.0).then_inc(ident_zero, 1)
            pool.wait_ge(ident_zero, 1)
            nc.gpsimd.affine_select(out=ident[:], in_=ident[:], compare_op=ALU.not_equal, fill=1.0,
                                    base=0, pattern=[[-1, P]], channel_multiplier=1).then_inc(ident_ready, 1)
            pool.wait_ge(consts_ready, 1)
            for g in range(GROUPS):
                pool.wait_ge(var_ready, g + 1)
                nc.gpsimd.tensor_tensor(cols(first_rstd, g, BT), var_eps[:], minus_half[:], ALU.pow)\
                    .then_inc(rstd_ready, 1)
            for e in range(EXPERTS):
                nc.gpsimd.memset(rank[:, :, e], float(EXPERTS - e)).then_inc(consts_ready, 1)
            nc.gpsimd.memset(ones[:], 1.0).then_inc(order_consts, 1)
            pool.wait_ge(order_consts, 1)
            nc.gpsimd.affine_select(out=before[:], in_=ones[:], compare_op=ALU.is_gt, fill=0.0,
                                    base=0, pattern=[[1, P]], channel_multiplier=-1).then_inc(order_consts, 1)
            nc.gpsimd.iota(order_int[:, 0:TILES], pattern=[[P, TILES]], base=0, channel_multiplier=0).then_inc(order_consts, 1)
            nc.gpsimd.iota(order_int[:, TILES:], pattern=[[1, SLOTS]], base=0, channel_multiplier=0).then_inc(order_consts, 1)
            nc.gpsimd.iota(position_int[:], pattern=[[CHOICES * P, TILES], [1, CHOICES]], base=0,
                           channel_multiplier=CHOICES).then_inc(order_consts, 1)
            pool.wait_ge(order_consts, 5)
            nc.gpsimd.tensor_copy(order[:], order_int[:]).then_inc(order_float, 1)
            nc.gpsimd.tensor_copy(meta[:, :, :, 0], position_int[:].rearrange("p (t k) -> p t k", k=CHOICES))\
                .then_inc(order_float, 1)
            nc.gpsimd.iota(rows_index[:], pattern=[[P, RING]], base=PICKS, channel_multiplier=1).then_inc(blank_step, 1)
            nc.gpsimd.memset(rows[:], 0.0).then_inc(blank_step, 1)
            pool.wait_ge(blank_step, 2)
            nc.gpsimd.tensor_copy(rows[:, :, D], rows_index[:]).then_inc(blank_ready, 1)

            def normalise(n, kind, half):
                pool.wait_ge(inv_ready, n + 1)
                pool.sem_inc(pool_turn, 1)
                for it in (2 * half, 2 * half + 1):
                    nc.gpsimd.tensor_scalar(probs[:, kind, it, :], probs[:, kind, it, :],
                                            inv_sum[:, kind, it:it + 1], 1.0, ALU.mult, ALU.mult)\
                        .then_inc(probs_ready, 1)

            def scatter_tokens(t, k):
                u = CHOICES * t + k
                if isinstance(t, int):
                    token, way_back = xn[:, t, :], meta[:, t, k, :]
                else:
                    token = xn[:, bass.ds(t, 1), :].rearrange("p o d -> p (o d)")
                    way_back = meta[:, bass.ds(t, 1), k, :].rearrange("p o c -> p (o c)")
                nc.gpsimd.tensor_copy(staged[:, 0:D], token).then_inc(staged_ready, 1)
                nc.gpsimd.tensor_copy(staged[:, D:ROW], way_back).then_inc(staged_ready, 1)
                nc.gpsimd.tensor_copy(staged_position[:], columns(position_int, u, 1)).then_inc(staged_ready, 1)
                pool.wait_ge(staged_ready, 3 * (u + 1))
                pool.sem_inc(pool_turn, 1)
                nc.gpsimd.indirect_dma_start(out=sorted_rows, out_offset=bass.IndirectOffsetOnAxis(ap=staged_position[:], axis=0),
                                             in_=staged[:], in_offset=None, bounds_check=RINGS * RING * P - 1)\
                    .then_inc(scattered, 16)

            def unit(u, scatter):
                n = STEPS * u
                normalise(n, A, 0)
                normalise(n + 1, A, 1)
                normalise(n + 2, B, 0)
                scatter()
                normalise(n + 3, B, 1)

            def staged_again(count):
                pool.wait_ge(scattered, 16 * count)
                pool.sem_inc(pool_turn, 1)

            def scatter_nothing():
                pass

            unit(0, scatter_nothing)
            unit(1, scatter_nothing)
            pool.wait_ge(positions_ready, 1)
            pool.wait_ge(blank_moved, 16 * RING)
            scatter_tokens(0, 0)

            with pool.Fori(1, TILES) as t:
                def second_choice():
                    staged_again(CHOICES * t - 1)
                    scatter_tokens(t - 1, 1)

                def first_choice():
                    staged_again(CHOICES * t)
                    scatter_tokens(t, 0)

                unit(CHOICES * t, second_choice)
                unit(CHOICES * t + 1, first_choice)

            staged_again(PICKS // P - 1)
            scatter_tokens(TILES - 1, 1)

            def return_rows(i, s, j):
                if s == 0 and not isinstance(i, int):
                    pool.wait_ge(fin_var_ready, j)
                    pool.sem_inc(pool_turn, 1)
                    nc.gpsimd.tensor_tensor(rstd[:, 0:2], var_eps[:, 0:2], minus_half[:, 0:2], ALU.pow)\
                        .then_inc(fin_rstd_ready, 1)
                if from_unit(i, 4):
                    pool.wait_ge(returned[s], 16 * j)
                    pool.sem_inc(pool_turn, 1)
                index = rows_meta[:, i, 0:1] if isinstance(i, int) else \
                    rows_meta[:, bass.ds(i, 1), 0:1].rearrange("p o c -> p (o c)")
                pool.wait_ge(rows_t_copied, i + 1)
                pool.sem_inc(pool_turn, 1)
                nc.gpsimd.tensor_copy(rows_index[:, s:s + 1], index).then_inc(index_ready, 1)
                pool.wait_ge(index_ready, i + 1)
                pool.wait_ge(result_ready, i + 1)
                pool.sem_inc(pool_turn, 1)
                nc.gpsimd.indirect_dma_start(out=results, out_offset=bass.IndirectOffsetOnAxis(ap=rows_index[:, s:s + 1], axis=0),
                                             in_=result[:, s, :], in_offset=None, bounds_check=PICKS + RING * P - 1)\
                    .then_inc(returned[s], 16)

            over_tiles(pool, return_rows)

            for g in range(GROUPS - 1):
                pool.wait_ge(tail_step, g + 1)
                nc.gpsimd.tensor_tensor(group(z, g), group(z, g), group(x, g), ALU.add).then_inc(fin_ready, 1)

        @block.scalar
        def _(act):
            def split_hi(part):
                act.wait_ge(wqkv_loaded[part], 16)
                pairs = SPLITS[part]
                nc.scalar.activation(wqk_split[:, pairs, :, 0, :], wqkv[:, pairs, 0:2, :], ACT.Copy)\
                    .then_inc(wqk_hi_ready, 1)

            def copy_hi(u, ready, b, hi, hi_ready):
                act.wait_ge(ready, u + 1)
                nc.scalar.activation(hi[:], misc[b][:], ACT.Copy).then_inc(hi_ready, 1)

            split_hi(0)
            for g in range(GROUPS):
                act.wait_ge(xnT_ready, g + 1)
                nc.scalar.activation(cols(xnT_hi, g, SEQ), score[:, g, :], ACT.Copy)
                nc.scalar.activation(cols(xnT, g, SEQ), score[:, g, :], ACT.Copy).then_inc(xnT_f32_ready, 1)
                if g == 1:
                    copy_hi(0, q_ready, Q_BANK[0], q_hi, q_hi_ready)
                    copy_hi(0, k_ready, K_BANK[0], k_hi, k_hi_ready)
            split_hi(1)

            def exps(n, kind, half):
                act.wait_ge(bias_ready, n + 1)
                if from_unit(n, STEPS):
                    act.wait_ge(probsT_ready, 2 * (n - STEPS + 1))
                for it in (2 * half, 2 * half + 1):
                    nc.scalar.activation(probs[:, kind, it, :], score[:, it, :], ACT.Exp,
                                         bias=exp_bias[:, kind, it:it + 1], scale=SCALE,
                                         accum_out=exp_sum[:, kind, it:it + 1]).then_inc(exp_ready, 1)

            def copy_probsT(n, u, slot, kind, half):
                if kind == A and half == 0 and from_unit(u, 2):
                    act.wait_ge(attn_ready, u - 1)
                it = 2 * half
                act.wait_ge(probsT_ready, 2 * n + 1)
                nc.scalar.activation(probsT[:, slot, kind, :, it * P:(it + 1) * P],
                                     tr_bank[0][:].rearrange("p (j i) -> p j i", i=P), ACT.Copy)\
                    .then_inc(copied_by_act, 1)

            def copy_attn(u, slot):
                act.wait_ge(attn_ready, u + 1)
                nc.scalar.activation(attnT[:], misc[PV_BANK[slot]][:], ACT.Copy).then_inc(attn_copied, 1)

            act.wait_ge(shifted_ready, 1)
            nc.scalar.activation(prob[:], left[:], ACT.Exp).then_inc(router_exp_ready, 1)

            def unit(u, slot, turn):
                nxt, n = 1 - slot, STEPS * u
                if from_unit(u, 2):
                    copy_attn(u - 2, slot)
                if not is_last(u, UNITS):
                    if is_first(u):
                        exps(n, A, 0)
                    for kind in (A, B):
                        act.wait_ge(stack_loaded[slot][kind], 16 * STACK_DMAS * (turn + 1))
                    copy_hi(u + 1, q_ready, Q_BANK[nxt], q_hi, q_hi_ready)
                if not is_first(u):
                    exps(n, A, 0)
                if from_unit(u, 1):
                    copy_probsT(n - 2, u - 1, nxt, B, 0)
                if not is_last(u, UNITS):
                    copy_hi(u + 1, k_ready, K_BANK[nxt], k_hi, k_hi_ready)
                if from_unit(u, 1):
                    copy_probsT(n - 1, u - 1, nxt, B, 1)
                exps(n + 1, A, 1)
                if is_first(u):
                    nc.scalar.activation(z[:], xn[:], ACT.Copy).then_inc(z_copied, 1)
                copy_probsT(n, u, slot, A, 0)
                exps(n + 2, B, 0)
                copy_probsT(n + 1, u, slot, A, 1)
                exps(n + 3, B, 1)

            over_units(act, unit)
            copy_attn(UNITS - 2, 0)
            copy_probsT(STEPS * UNITS - 2, UNITS - 1, 1, B, 0)
            copy_probsT(STEPS * UNITS - 1, UNITS - 1, 1, B, 1)
            copy_attn(UNITS - 1, 1)

            def copy_hidden_t(i, s):
                act.wait_ge(hidden_t_ready, i + 1)
                if from_unit(i, 2):
                    act.wait_ge(product_ready, i - 1)
                nc.scalar.activation(hidden_t[:, s % 2], hidden_bank[:, 0:NC * P].rearrange("p (c t) -> p c t", c=NC),
                                     ACT.Copy).then_inc(hidden_t_copied, 1)

            def tile(i, s, j):
                act.wait_ge(gate_ready, i + 1)
                if from_unit(i, 2):
                    act.wait_ge(hidden_ready, i - 1)
                nc.scalar.activation(gate_act[:, s % 2, :], gate_bank[s % 2][:, 0:INTER], ACT.Silu).then_inc(silu_ready, 1)
                if from_unit(i, 1):
                    copy_hidden_t(i - 1, s + 1)

            over_tiles(act, tile)
            copy_hidden_t(SLOTS - 1, SLOTS - 1)

            for g in range(GROUPS):
                act.wait_ge(summed_ready, g + 1)
                nc.scalar.activation(group(xn, g), group(xn, g), ACT.Silu).then_inc(gate_silu_ready, 1)

        @block.vector
        def _(dve):
            def scale_group(g):
                dve.wait_ge(rstd_ready, g + 1)
                for t in range(BT):
                    tile = g * BT + t
                    last = nc.vector.tensor_scalar(xn[:, tile, :], x[:, tile, :], first_mean_var[:, g, t, 0:1],
                                                   first_rstd[:, tile:tile + 1], ALU.subtract, ALU.mult)
                last.then_inc(xn_ready, 1)

            def statistics(g):
                dve.wait_ge(x_loaded[g], 16)
                for t in range(BT):
                    last = nc.vector.bn_stats(stats[:, t, :], x[:, g * BT + t, :])
                last.then_inc(stat_step, 1)
                dve.wait_ge(stat_step, 2 * g + 1)
                for t in range(BT):
                    last = nc.vector.bn_aggr(first_mean_var[:, g, t, :], stats[:, t, :])
                last.then_inc(stat_step, 1)
                dve.wait_ge(stat_step, 2 * g + 2)
                if g >= 1:
                    dve.wait_ge(rstd_ready, g)
                nc.vector.tensor_scalar(var_eps[:], first_mean_var[:, g, :, 1], 1.0, LN_EPS, ALU.mult, ALU.add)\
                    .then_inc(var_ready, 1)

            def tokens_lo(g):
                dve.wait_ge(xnT_f32_ready, g + 1)
                nc.vector.tensor_tensor(cols(xnT_lo, g, SEQ), score[:, g, :], cols(xnT_hi, g, SEQ).bitcast(F32),
                                        ALU.subtract).then_inc(xnT_lo_ready, 1)

            def split_lo(part):
                dve.wait_ge(wqk_hi_ready, part + 1)
                pairs = SPLITS[part]
                nc.vector.tensor_tensor(wqk_split[:, pairs, :, 1, :], wqkv[:, pairs, 0:2, :],
                                        wqk_split[:, pairs, :, 0, :].bitcast(F32), ALU.subtract).then_inc(wqk_lo_ready, 1)

            def copy_lo(u, ready_hi, hi, lo, lo_ready, b):
                dve.wait_ge(ready_hi, u + 1)
                nc.vector.tensor_tensor(lo[:], misc[b][:], hi[:].bitcast(F32), ALU.subtract).then_inc(lo_ready, 1)

            statistics(0)
            statistics(1)
            scale_group(0)
            statistics(2)
            scale_group(1)
            split_lo(0)
            tokens_lo(0)
            statistics(3)
            scale_group(2)
            copy_lo(0, q_hi_ready, q_hi, q_lo, q_lo_ready, Q_BANK[0])
            copy_lo(0, k_hi_ready, k_hi, k_lo, k_lo_ready, K_BANK[0])
            scale_group(3)
            for g in range(1, GROUPS):
                tokens_lo(g)

            step = [0]

            def link(instruction):
                step[0] += 1
                instruction.then_inc(route_step, 1)
                dve.wait_ge(route_step, step[0])

            lg = logits_bank[:, 0:TILES * EXPERTS].rearrange("p (t e) -> p t e", e=EXPERTS)
            dve.wait_ge(logits_ready, GROUPS)
            link(nc.vector.reduce_max(best[:], lg, AX_X))
            nc.vector.tensor_tensor(left[:], lg, spread(best[:], EXPERTS), ALU.subtract).then_inc(shifted_ready, 1)

            def pick(values, out):
                link(nc.vector.reduce_max(best[:], values, AX_X))
                link(nc.vector.tensor_tensor(eq[:], values, spread(best[:], EXPERTS), ALU.is_equal))
                link(nc.vector.tensor_tensor(eq[:], eq[:], rank[:], ALU.mult))
                link(nc.vector.reduce_max(best[:], eq[:], AX_X))
                link(nc.vector.tensor_tensor(out, eq[:], spread(best[:], EXPERTS), ALU.is_equal))

            def route():
                dve.wait_ge(router_exp_ready, 1)
                link(nc.vector.reduce_sum(best[:], prob[:], AX_X))
                link(nc.vector.reciprocal(best[:], best[:]))
                link(nc.vector.tensor_tensor(prob[:], prob[:], spread(best[:], EXPERTS), ALU.mult))
                dve.wait_ge(consts_ready, 1 + EXPERTS)
                pick(prob[:], chosen[:, 0])
                link(nc.vector.scalar_tensor_tensor(out=left[:], in0=chosen[:, 0], scalar=-2.0, in1=prob[:],
                                                    op0=ALU.mult, op1=ALU.add))

            def route_second():
                pick(left[:], chosen[:, 1])
                link(nc.vector.tensor_tensor(both[:], chosen[:, 0], chosen[:, 1], ALU.add))

            def running_sums():
                src, turn, shift = both[:], 0, 1
                while shift < TILES:
                    dst = running[:, turn]
                    nc.vector.tensor_copy(dst[:, 0:shift], src[:, 0:shift])
                    link(nc.vector.tensor_tensor(dst[:, shift:], src[:, shift:], src[:, 0:TILES - shift], ALU.add))
                    src, turn, shift = dst, 1 - turn, 2 * shift
                nc.vector.tensor_tensor(left[:], src, both[:], ALU.subtract).then_inc(running_ready, 1)

            def places():
                dve.wait_ge(order_read, 1)
                dve.wait_ge(order_float, 2)
                ranks = counted[:, 0:TILES * EXPERTS].rearrange("p (t e) -> p t e", e=EXPERTS)
                counts = counted[:, TILES * EXPERTS:(TILES + 1) * EXPERTS]
                link(nc.vector.tensor_tensor(above[:, 0:TILES, :], counts.unsqueeze(1).to_broadcast([P, TILES, EXPERTS]),
                                             spread(order[:, 0:TILES], EXPERTS), ALU.is_gt))
                link(nc.vector.reduce_sum(tiles_of[:], above[:, 0:TILES, :].rearrange("p j e -> p e j"), AX_X))
                src, turn, shift = tiles_of[:], 0, 1
                while shift < EXPERTS:
                    dst = ends[:, turn]
                    nc.vector.tensor_copy(dst[:, 0:shift], src[:, 0:shift])
                    link(nc.vector.tensor_tensor(dst[:, shift:], src[:, shift:], src[:, 0:EXPERTS - shift], ALU.add))
                    src, turn, shift = dst, 1 - turn, 2 * shift
                start = best[:, 0:EXPERTS]
                link(nc.vector.tensor_tensor(start, src, tiles_of[:], ALU.subtract))
                link(nc.vector.scalar_tensor_tensor(out=place[:], in0=start.unsqueeze(1).to_broadcast([P, TILES, EXPERTS]),
                                                    scalar=float(P), in1=ranks, op0=ALU.mult, op1=ALU.add))

            def positions():
                for k in range(CHOICES):
                    link(nc.vector.tensor_tensor(eq[:], prob[:], chosen[:, k], ALU.mult))
                    link(nc.vector.reduce_sum(meta[:, :, k, 1], eq[:], AX_X))
                    link(nc.vector.tensor_tensor(eq[:], place[:], chosen[:, k], ALU.mult))
                    link(nc.vector.reduce_sum(position[:, :, k], eq[:], AX_X))
                nc.vector.tensor_copy(position_int[:], position[:].rearrange("p t k -> p (t k)")).then_inc(positions_ready, 1)

            def tile_experts():
                last_ends = ends[:, 0]
                link(nc.vector.tensor_tensor(above[:], last_ends.unsqueeze(1).to_broadcast([P, SLOTS, EXPERTS]),
                                             spread(order[:, TILES:], EXPERTS), ALU.is_le))
                link(nc.vector.reduce_sum(expert_of[:], above[:], AX_X))
                link(nc.vector.tensor_scalar(expert_of[:], expert_of[:], float(EXPERTS - 1), None, ALU.min))
                nc.vector.tensor_copy(expert_int[:, 0:2], expert_of[:, 0:2])
                nc.vector.scalar_tensor_tensor(out=expert_int[:, 2:], in0=expert_of[:, 0:SLOTS - 2], scalar=float(EXPERTS),
                                               in1=expert_of[:, 2:], op0=ALU.mult, op1=ALU.add).then_inc(experts_ready, 1)

            def maxima(n, kind, half):
                its = slice(2 * half, 2 * half + 2)
                dve.wait_ge(scores_ready, 2 * (n + 1))
                nc.vector.reduce_max(row_max[:, kind, its], score[:, its, :], AX_X).then_inc(max_ready, 1)
                dve.wait_ge(max_ready, n + 1)
                nc.vector.tensor_scalar(exp_bias[:, kind, its], row_max[:, kind, its], -SCALE, None, ALU.mult)\
                    .then_inc(bias_ready, 1)

            def inverse(n, kind, half):
                its = slice(2 * half, 2 * half + 2)
                dve.wait_ge(exp_ready, 2 * (n + 1))
                nc.vector.reciprocal(inv_sum[:, kind, its], exp_sum[:, kind, its]).then_inc(inv_ready, 1)

            def copy_v(u, slot):
                dve.wait_ge(v_ready, u + 1)
                nc.vector.tensor_copy(v_unit[:, slot].rearrange("p t c -> p (t c)"), misc[V_BANK[slot]][:])\
                    .then_inc(v_copied, 1)

            def copy_probsT(n, u, slot, kind, half):
                if kind == A and half == 0 and from_unit(u, 2):
                    dve.wait_ge(attn_ready, u - 1)
                it = 2 * half + 1
                dve.wait_ge(probsT_ready, 2 * n + 2)
                nc.vector.tensor_copy(probsT[:, slot, kind, :, it * P:(it + 1) * P],
                                      tr_bank[1][:].rearrange("p (j i) -> p j i", i=P)).then_inc(copied_by_dve, 1)

            def add_proj(u, slot):
                if is_first(u):
                    dve.wait_ge(z_copied, 1)
                dve.wait_ge(proj_ready, u + 1)
                to = group(z, u // PAIRS)
                nc.vector.tensor_tensor(to, misc[PROJ_BANK[slot]][:].rearrange("p (t d) -> p t d", d=D), to, ALU.add)\
                    .then_inc(proj_added, 1)

            split_lo(1)

            def unit(u, slot, turn):
                nxt, n = 1 - slot, STEPS * u
                if from_unit(u, 1):
                    inverse(n - 1, B, 1)
                maxima(n, A, 0)
                if not is_last(u, UNITS):
                    copy_lo(u + 1, q_hi_ready, q_hi, q_lo, q_lo_ready, Q_BANK[nxt])
                if from_unit(u, 1):
                    copy_probsT(n - 2, u - 1, nxt, B, 0)
                inverse(n, A, 0)
                maxima(n + 1, A, 1)
                if not is_last(u, UNITS):
                    copy_lo(u + 1, k_hi_ready, k_hi, k_lo, k_lo_ready, K_BANK[nxt])
                if is_first(u):
                    route()
                copy_v(u, slot)
                if from_unit(u, 1):
                    copy_probsT(n - 1, u - 1, nxt, B, 1)
                inverse(n + 1, A, 1)
                maxima(n + 2, B, 0)
                if is_first(u):
                    route_second()
                    running_sums()
                if is_last(u, 2):
                    dve.wait_ge(order_counted, 1)
                    nc.vector.tensor_copy(counted[:], misc[PROJ_BANK[1]][:, 0:(TILES + 1) * EXPERTS]).then_inc(order_read, 1)
                if from_unit(u, 2):
                    add_proj(u - 2, slot)
                copy_probsT(n, u, slot, A, 0)
                inverse(n + 2, B, 0)
                maxima(n + 3, B, 1)
                if is_last(u, 2):
                    places()
                    positions()
                if is_last(u, UNITS - 1):
                    tile_experts()
                copy_probsT(n + 1, u, slot, A, 1)

            over_units(dve, unit)
            inverse(STEPS * UNITS - 1, B, 1)
            copy_probsT(STEPS * UNITS - 2, UNITS - 1, 1, B, 0)
            copy_probsT(STEPS * UNITS - 1, UNITS - 1, 1, B, 1)
            add_proj(UNITS - 2, 0)

            def copy_rows_t(i, s):
                dve.wait_ge(rows_t_ready, i + 1)
                if from_unit(i, 2):
                    dve.wait_ge(up_ready, i - 1)
                of_tile = rows_meta[:, i, :] if isinstance(i, int) else rows_meta[:, bass.ds(i, 1), :].rearrange("p o c -> p (o c)")
                nc.vector.tensor_copy(of_tile, rows[:, s % 4, D:ROW])
                nc.vector.tensor_copy(rows_t[:, s % 2, :], rows_bank[:, 0:P]).then_inc(rows_t_copied, 1)

            def scale_result(i, s, j):
                dve.wait_ge(product_ready, i + 1)
                if from_unit(i, 4):
                    dve.wait_ge(returned[s], 16 * j)
                w = rows_meta[:, i, 1:2] if isinstance(i, int) else \
                    rows_meta[:, bass.ds(i, 1), 1:2].rearrange("p o c -> p (o c)")
                nc.vector.tensor_scalar(result[:, s, :], result_bank[s % 2][:, 0:D], w, None, ALU.mult).then_inc(result_ready, 1)

            def normalise_z(s, j):
                two = z[:, bass.ds(2 * (j - 1), 2), :]
                def one(t):
                    return z[:, bass.ds(2 * (j - 1) + t, 1), :].rearrange("p o d -> p (o d)")

                def after(count):
                    dve.wait_ge(fin_step, LN_STEPS * (j - 1) + count)
                    dve.sem_inc(dve_turn, 1)
                if s == 0:
                    for t in range(2):
                        last = nc.vector.bn_stats(stats[:, t, :], one(t))
                    last.then_inc(fin_step, 1)
                elif s == 1:
                    after(1)
                    for t in range(2):
                        last = nc.vector.bn_aggr(mean_var[:, t, :], stats[:, t, :])
                    last.then_inc(fin_step, 1)
                    after(2)
                    nc.vector.tensor_scalar(var_eps[:, 0:2], mean_var[:, 0:2, 1], 1.0, LN_EPS, ALU.mult, ALU.add)\
                        .then_inc(fin_var_ready, 1)
                elif s == 3:
                    dve.wait_ge(fin_rstd_ready, j)
                    dve.sem_inc(dve_turn, 1)
                    for t in range(2):
                        last = nc.vector.tensor_scalar(one(t), one(t), mean_var[:, t, 0:1], rstd[:, t:t + 1],
                                                       ALU.subtract, ALU.mult)
                    last.then_inc(fin_step, 1)
                    after(3)
                    nc.vector.tensor_tensor(two, two, gamma[:].unsqueeze(1).to_broadcast([P, 2, D]), ALU.mult)\
                        .then_inc(fin_step, 1)
                    after(4)
                    nc.vector.tensor_tensor(two, two, beta[:].unsqueeze(1).to_broadcast([P, 2, D]), ALU.add)

            def tile(i, s, j):
                if not is_last(i, SLOTS):
                    copy_rows_t(i + 1, s + 1)
                dve.wait_ge(up_ready, i + 1)
                dve.wait_ge(silu_ready, i + 1)
                if from_unit(i, 2):
                    dve.wait_ge(hidden_t_ready, i - 1)
                nc.vector.tensor_tensor(hidden[:, s % 2, :], up_bank[s % 2][:, 0:INTER], gate_act[:, s % 2, :], ALU.mult)\
                    .then_inc(hidden_ready, 1)
                if is_first(i):
                    dve.wait_ge(proj_added, UNITS - 1)
                    add_proj(UNITS - 1, 1)
                    dve.wait_ge(proj_added, UNITS)
                    dve.wait_ge(const_loaded, 32)
                if from_unit(i, 2):
                    scale_result(i - 2, (s + 2) % 4, j if s >= 2 else j - 1)
                if not isinstance(i, int):
                    normalise_z(s, j)

            copy_rows_t(0, 0)
            over_tiles(dve, tile)
            for i in (SLOTS - 2, SLOTS - 1):
                scale_result(i, i % 4, i // 4)

            def add_results(g):
                dve.wait_ge(picked_loaded[g], 16)
                two = picked[:, g * BT:(g + 1) * BT]
                nc.vector.tensor_tensor(group(xn, g), two[:, :, 0, :], two[:, :, 1, :], ALU.add).then_inc(summed_ready, 1)

            def finish(g):
                dve.wait_ge(gate_silu_ready, g + 1)
                nc.vector.tensor_tensor(group(z, g), group(z, g), group(xn, g), ALU.mult).then_inc(tail_step, 1)
                if g == GROUPS - 1:
                    dve.wait_ge(tail_step, g + 1)
                    nc.vector.tensor_tensor(group(z, g), group(z, g), group(x, g), ALU.add).then_inc(last_fin_ready, 1)

            for g in range(GROUPS):
                add_results(g)
                if g >= 1:
                    finish(g - 1)
            finish(GROUPS - 1)

        @block.tensor
        def _(pe):
            def split_matmul(dst, w_hi, w_lo, m_hi, m_lo):
                nc.tensor.matmul(dst, w_hi, m_hi, start=True, stop=False)
                nc.tensor.matmul(dst, w_hi, m_lo, start=False, stop=False)
                return nc.tensor.matmul(dst, w_lo, m_hi, start=False, stop=True)

            def project(u, slot, turn, part, b, ready, at):
                if part == 0:
                    pe.wait_ge(unit_loaded[slot], 32 * (turn + 1))
                w = w_unit[:, slot, part]
                split_matmul(misc[b][:], w[:, 0, :], w[:, 1, :], columns(xnT_hi, at, SEQ), columns(xnT_lo, at, SEQ))\
                    .then_inc(ready, 1)

            def logits(g):
                pe.wait_ge(xnT_f32_ready, g + 1)
                for t in range(g * BT, (g + 1) * BT):
                    last = nc.tensor.matmul(logits_bank[:, t * EXPERTS:(t + 1) * EXPERTS], xnT[:, t * P:(t + 1) * P],
                                            router[:], start=True, stop=True)
                last.then_inc(logits_ready, 1)

            pe.wait_ge(ident_ready, 1)
            for g in range(GROUPS):
                pe.wait_ge(xn_ready, g + 1)
                for t in range(BT):
                    last = nc.tensor.transpose(score[:, g, t * P:(t + 1) * P], xn[:, g * BT + t, :], ident[:])
                last.then_inc(xnT_ready, 1)
                if g == 0:
                    pe.wait_ge(router_loaded, 16)
                else:
                    logits(g - 1)
                if g == 1:
                    pe.wait_ge(xnT_lo_ready, 1)
                    project(0, 0, 0, 0, Q_BANK[0], q_ready, 0)
                    project(0, 0, 0, 1, K_BANK[0], k_ready, 0)
            logits(GROUPS - 1)
            pe.wait_ge(xnT_lo_ready, GROUPS)

            def early(value):
                if not isinstance(value, int):
                    pe.compute_val(value)
                return value

            def project_v(u, slot, b, at):
                w = columns(wqkv_flat, at, P)
                for jt in range(BT):
                    last = nc.tensor.matmul(misc[b][:, jt * P:(jt + 1) * P], x_unit[:, slot, jt * P:(jt + 1) * P], w,
                                            start=True, stop=True)
                last.then_inc(v_ready, 1)

            def scores(n, kind, half, slot, turn):
                if half == 0:
                    pe.wait_ge(stack_loaded[slot][kind], 16 * STACK_DMAS * (turn + 1))
                if from_unit(n, 2):
                    pe.wait_ge(exp_ready, 2 * (n - 1))
                for it in (2 * half, 2 * half + 1):
                    q = q_stack[:, slot, kind, it * P:(it + 1) * P]
                    nc.tensor.matmul(score[:, it, :], q, k_hi_stack[:, slot, kind, :], start=True, stop=False)
                    nc.tensor.matmul(score[:, it, :], q, k_lo_stack[:, slot, kind, :], start=False, stop=True)\
                        .then_inc(scores_ready, 1)

            def transposes(n, kind, half):
                if is_first(n):
                    pe.wait_ge(shifted_ready, 1)
                for j, copied in ((0, copied_by_act), (1, copied_by_dve)):
                    it = 2 * half + j
                    pe.wait_ge(probs_ready, 2 * n + j + 1)
                    if from_unit(n, 1):
                        pe.wait_ge(copied, n)
                    for jt in range(BT):
                        last = nc.tensor.transpose(tr_bank[j][:, jt * P:(jt + 1) * P],
                                                   probs[:, kind, it, jt * P:(jt + 1) * P], ident[:])
                    last.then_inc(probsT_ready, 1)

            def attend(u, slot, key_tiles):
                if key_tiles[0] == 0:
                    pe.wait_ge(v_copied, u + 1)
                    pe.wait_ge(copied_by_act, STEPS * (u + 1))
                    pe.wait_ge(copied_by_dve, STEPS * (u + 1))
                for jt in key_tiles:
                    for kind in (A, B):
                        last = nc.tensor.matmul(misc[PV_BANK[slot]][kind * DH:(kind + 1) * DH, :],
                                                v_unit[:, slot, jt, kind * DH:(kind + 1) * DH],
                                                probsT[:, slot, kind, jt, :], start=jt == 0, stop=jt == BT - 1)
                if key_tiles[-1] == BT - 1:
                    last.then_inc(attn_ready, 1)

            def out_project(u, b, at):
                pe.wait_ge(attn_copied, u + 1)
                w = columns(wo_flat, at, D)
                for it in range(BT):
                    last = nc.tensor.matmul(misc[b][:, it * D:(it + 1) * D], attnT[:, it * P:(it + 1) * P], w,
                                            start=True, stop=True)
                last.then_inc(proj_ready, 1)

            def count():
                pe.wait_ge(order_consts, 2)
                pe.wait_ge(running_ready, 1)
                order_bank = misc[PROJ_BANK[1]]
                ranks, counts = order_bank[:, 0:TILES * EXPERTS], order_bank[:, TILES * EXPERTS:(TILES + 1) * EXPERTS]
                nc.tensor.matmul(ranks, before[:], both[:].rearrange("p t e -> p (t e)"), start=True, stop=False)
                nc.tensor.matmul(ranks, ones[:], left[:].rearrange("p t e -> p (t e)"), start=False, stop=True)
                nc.tensor.matmul(counts, ones[:], running[:, 1, TILES - 1, :], start=True, stop=True)\
                    .then_inc(order_counted, 1)

            def unit(u, slot, turn):
                more = not is_last(u, UNITS)
                nxt, n = 1 - slot, STEPS * u
                next_tokens = early((u + 1) // PAIRS * SEQ)
                v_weights = early(u % PAIRS * (3 * P) + 2 * P)
                out_weights = early((u - 2) % PAIRS * D) if from_unit(u, 2) else None
                scores(n, A, 0, slot, turn)
                if more:
                    if is_first(u):
                        pe.wait_ge(k_lo_ready, 1)
                    project(u + 1, nxt, turn + slot, 0, Q_BANK[nxt], q_ready, next_tokens)
                    if from_unit(u, 2):
                        pe.wait_ge(attn_copied, u - 1)
                    else:
                        pe.wait_ge(*((v_copied, 1) if u else (q_lo_ready, 1)))
                    project(u + 1, nxt, turn + slot, 1, K_BANK[nxt], k_ready, next_tokens)
                if from_unit(u, 1):
                    transposes(n - 2, B, 0)
                scores(n + 1, A, 1, slot, turn)
                if more:
                    pe.wait_ge(q_lo_ready, u + 2)
                else:
                    pe.wait_ge(proj_added, u - 2)
                project_v(u, slot, V_BANK[slot], v_weights)
                if from_unit(u, 1):
                    transposes(n - 1, B, 1)
                scores(n + 2, B, 0, slot, turn)
                if is_last(u, 2):
                    pe.wait_ge(k_lo_ready, u + 2)
                    count()
                if from_unit(u, 2):
                    if more:
                        pe.wait_ge(k_lo_ready, u + 2)
                    out_project(u - 2, PROJ_BANK[slot], out_weights)
                transposes(n, A, 0)
                if from_unit(u, 1):
                    pe.wait_ge(v_copied, u + 1)
                    attend(u - 1, nxt, (0, 1))
                scores(n + 3, B, 1, slot, turn)
                transposes(n + 1, A, 1)
                if from_unit(u, 1):
                    attend(u - 1, nxt, (2, 3))
                if is_last(u, 2):
                    pe.wait_ge(wo_loaded, 16)
                    pe.wait_ge(order_read, 1)

            over_units(pe, unit)
            transposes(STEPS * UNITS - 2, B, 0)
            transposes(STEPS * UNITS - 1, B, 1)
            out_project(UNITS - 2, PROJ_BANK[0], (UNITS - 2) % PAIRS * D)
            pe.wait_ge(proj_added, UNITS - 2)
            attend(UNITS - 1, 1, range(BT))

            def experts(i):
                return nc.tensor.value_load(expert_int[0:1, i:i + 1] if isinstance(i, int) else expert_int[0:1, bass.ds(i, 1)],
                                            min_val=0, max_val=EXPERTS * EXPERTS - 1)

            def transpose_rows(i, s, j):
                pe.wait_ge(rows_loaded[s], 16 * (j + 1))
                if from_unit(i, 1):
                    pe.wait_ge(rows_t_copied, i)
                nc.tensor.transpose(rows_bank[:, 0:P], rows[:, s, 0:D], ident[:]).then_inc(rows_t_ready, 1)

            def gate_and_up(i, s, at):
                pe.wait_ge(rows_t_copied, i + 1)
                if from_unit(i, 2):
                    pe.wait_ge(hidden_ready, i - 1)
                for weights, dst, ready in ((gate_w, gate_bank[s % 2], gate_ready), (up_w, up_bank[s % 2], up_ready)):
                    nc.tensor.matmul(dst[:, 0:INTER], rows_t[:, s % 2, :], columns(weights, at, INTER), start=True, stop=True).then_inc(ready, 1)

            def transpose_hidden(i, s):
                pe.wait_ge(hidden_ready, i + 1)
                if from_unit(i, 1):
                    pe.wait_ge(hidden_t_copied, i)
                for c in range(NC):
                    last = nc.tensor.transpose(hidden_bank[0:CHUNKS[c], c * P:(c + 1) * P],
                                               hidden[:, s % 2, c * P:c * P + CHUNKS[c]], ident[:])
                last.then_inc(hidden_t_ready, 1)

            def down_product(i, s, at):
                pe.wait_ge(hidden_t_copied, i + 1)
                if from_unit(i, 2):
                    pe.wait_ge(result_ready, i - 1)
                for c in range(NC):
                    m = CHUNKS[c]
                    last = nc.tensor.matmul(result_bank[s % 2][:, 0:D], hidden_t[0:m, s % 2, c, :],
                                            down_flat[0:m, bass.ds(at + c * D, D)],
                                            start=c == 0, stop=c == NC - 1)
                last.then_inc(product_ready, 1)

            def tile(i, s, j):
                both_experts = experts(i)
                at = early(both_experts % EXPERTS * INTER)
                if from_unit(i, 2):
                    down_at = early(both_experts // EXPERTS * (NC * D))
                if not is_last(i, SLOTS):
                    transpose_rows(i + 1, (s + 1) % 4, j + (s + 1) // 4)
                gate_and_up(i, s, at)
                if is_first(i):
                    out_project(UNITS - 1, PROJ_BANK[1], (UNITS - 1) % PAIRS * D)
                if from_unit(i, 1):
                    if is_last(i, 2):
                        pe.wait_ge(proj_added, UNITS)
                    transpose_hidden(i - 1, s + 1)
                if from_unit(i, 2):
                    down_product(i - 2, s, down_at)

            pe.wait_ge(proj_added, UNITS - 1)
            transpose_rows(0, 0, 0)
            pe.wait_ge(experts_ready, 1)
            pe.wait_ge(gate_up_loaded, 32)
            pe.wait_ge(down_loaded, 16 * NC)
            over_tiles(pe, tile)
            down_product(SLOTS - 2, SLOTS - 2, early(experts(SLOTS - 2) % EXPERTS * (NC * D)))
            transpose_hidden(SLOTS - 1, SLOTS - 1)
            down_product(SLOTS - 1, SLOTS - 1, early(experts(SLOTS - 1) % EXPERTS * (NC * D)))


Q_BANK = [1, 0]
K_BANK = [0, 1]
V_BANK = [0, 1]
PROJ_BANK = [1, 0]
PV_BANK = [1, 0]
STACK_DMAS = 6
LN_STEPS = 4


def kernel(L0_attn_h, L0_attn_Wq, L0_attn_Wk, L0_attn_Wv, L0_attn_Wo, L0_attn_gamma, L0_attn_beta,
           L0_ffn_router_w, L0_ffn_gate_w, L0_ffn_up_w, L0_ffn_down_w):
    import numpy as np
    import concourse.bacc as bacc
    from concourse.bass_utils import run_bass_kernel_spmd

    def tiles(a):
        return np.asarray(a).reshape(TILES, P, D).transpose(1, 0, 2)

    def pairs(w):
        return np.asarray(w).reshape(D, PAIRS, P)

    arrays = {
        "x_in": tiles(L0_attn_h),
        "wqkv_in": np.stack([pairs(L0_attn_Wq), pairs(L0_attn_Wk), pairs(L0_attn_Wv)], axis=2),
        "wo_in": np.asarray(L0_attn_Wo).reshape(PAIRS, P, D).transpose(1, 0, 2),
        "gamma_in": np.asarray(L0_attn_gamma),
        "beta_in": np.asarray(L0_attn_beta),
        "router_in": np.asarray(L0_ffn_router_w).T,
        "gate_up_in": np.concatenate([np.asarray(L0_ffn_gate_w), np.asarray(L0_ffn_up_w)], axis=1).transpose(0, 2, 1),
        "down_in": np.asarray(L0_ffn_down_w).transpose(0, 2, 1).reshape(EXPERTS * INTER, D),
    }
    arrays = {name: np.ascontiguousarray(a) for name, a in arrays.items()}
    nc = bacc.Bacc("TRN2", target_bir_lowering=False, num_devices=1)
    args = [nc.dram_tensor(name, a.shape, mybir.dt.from_np(a.dtype), kind="ExternalInput").ap()
            for name, a in arrays.items()]
    out = nc.dram_tensor("out", (P, TILES, D), F32, kind="ExternalOutput").ap()
    program(nc, *args, out)
    result = run_bass_kernel_spmd(nc, [arrays], core_ids=[0])
    y = result.results[0]["out"]
    return y.transpose(1, 0, 2).reshape(BATCH, SEQ, D)
```
